# Optimizing a Trainium2 kernel written in Bass

```python
import numpy as np
import jax
import jax.numpy as jnp

def _softmax(x, axis=-1):
    return jax.nn.softmax(x, axis=axis)

def _gelu(x):
    return jax.nn.gelu(x, approximate=True)

def _silu(x):
    return jax.nn.silu(x)

def _sigmoid(x):
    return jax.nn.sigmoid(x)

def _layernorm(x, axis=-1, eps=1e-05):
    m = jnp.mean(x, axis=axis, keepdims=True)
    v = jnp.var(x, axis=axis, keepdims=True)
    return (x - m) / jnp.sqrt(v + eps)

def _scatter_add(tgt, idx, src, axis=0):
    return tgt.at[idx].add(src)

def _segment_sum(src, seg, n):
    return jax.ops.segment_sum(src, seg, n)
kernel_name = 'mk_prb_d2_jaxref_r8_bd7df1'

def setup_inputs(seed: int=0):
    np.random.seed(seed)
    _w = jnp.asarray

    def _L0_attn_setup():
        import jax, jax.numpy as jnp
        import numpy as np
        EMBED_DIM = 128
        NUM_HEADS = 16
        HEAD_DIM = EMBED_DIM // NUM_HEADS
        key = jax.random.key(seed)
        ks = jax.random.split(key, 9)
        B, T, C = (2, 256, EMBED_DIM)
        s = 1.0 / np.sqrt(C)
        return {'x': jax.random.normal(ks[0], (B, T, C), dtype=jnp.float32), 'Wq': jax.random.normal(ks[1], (C, C), dtype=jnp.float32) * s, 'bq': jnp.zeros((C,), jnp.float32), 'Wk': jax.random.normal(ks[2], (C, C), dtype=jnp.float32) * s, 'bk': jnp.zeros((C,), jnp.float32), 'Wv': jax.random.normal(ks[3], (C, C), dtype=jnp.float32) * s, 'bv': jnp.zeros((C,), jnp.float32), 'Wo': jax.random.normal(ks[4], (C, C), dtype=jnp.float32) * s, 'bo': jnp.zeros((C,), jnp.float32)}
    _L0_attn_in = _L0_attn_setup()

    def _L0_ffn_setup():
        import jax, jax.numpy as jnp
        import numpy as np
        K = 2
        CAP_FACTOR = 1.25
        key = jax.random.key(seed)
        ks = jax.random.split(key, 6)
        B, T, C, H, E = (8, 256, 128, 512, 8)
        return {'x': jax.random.normal(ks[0], (B, T, C), dtype=jnp.float32), 'Wr': jax.random.normal(ks[1], (C, E), dtype=jnp.float32) * 0.02, 'W1': jax.random.normal(ks[2], (E, C, H), dtype=jnp.float32) * 0.02, 'b1': jax.random.normal(ks[3], (E, H), dtype=jnp.float32) * 0.02, 'W2': jax.random.normal(ks[4], (E, H, C), dtype=jnp.float32) * 0.02, 'b2': jax.random.normal(ks[5], (E, C), dtype=jnp.float32) * 0.02}
    _L0_ffn_in = _L0_ffn_setup()

    def _L1_attn_setup():
        import jax, jax.numpy as jnp
        import numpy as np
        DIM, NH, NKV = (128, 16, 4)
        HD = DIM // NH
        B, T = (2, 256)

        def _rotary_freqs(seq_len, dim):
            inv_freq = 1.0 / 10000.0 ** (jnp.arange(0, dim, 2, dtype=jnp.float32) / dim)
            pos = jnp.arange(seq_len, dtype=jnp.float32)
            return pos[:, None] * inv_freq[None, :]

        def _apply_rotary(x, freqs):
            x1, x2 = (x[..., ::2], x[..., 1::2])
            cos, sin = (jnp.cos(freqs), jnp.sin(freqs))
            return jnp.concatenate([x1 * cos - x2 * sin, x1 * sin - x2 * cos], axis=-1)
        key = jax.random.key(seed)
        ks = jax.random.split(key, 5)
        s = 0.02
        return {'x': jax.random.normal(ks[0], (B, T, DIM), dtype=jnp.float32), 'Wq': jax.random.normal(ks[1], (DIM, DIM), dtype=jnp.float32) * s, 'bq': jnp.zeros((DIM,), jnp.float32), 'Wk': jax.random.normal(ks[2], (DIM, NKV * HD), dtype=jnp.float32) * s, 'bk': jnp.zeros((NKV * HD,), jnp.float32), 'Wv': jax.random.normal(ks[3], (DIM, NKV * HD), dtype=jnp.float32) * s, 'bv': jnp.zeros((NKV * HD,), jnp.float32), 'Wo': jax.random.normal(ks[4], (DIM, DIM), dtype=jnp.float32) * s, 'bo': jnp.zeros((DIM,), jnp.float32)}
    _L1_attn_in = _L1_attn_setup()

    def _L1_ffn_setup():
        import jax, jax.numpy as jnp
        import numpy as np
        HIDDEN = 128
        INTER = 512
        NUM_EXPERTS = 8
        TOP_K = 2
        LN_EPS = 1e-05
        key = jax.random.key(seed)
        ks = jax.random.split(key, 8)
        B, S = (4, 256)
        scale = 0.02
        return {'hidden_states': jax.random.normal(ks[0], (B, S, HIDDEN), dtype=jnp.float32), 'ln_scale': jnp.ones((HIDDEN,), jnp.float32), 'ln_bias': jnp.zeros((HIDDEN,), jnp.float32), 'router_w': jax.random.normal(ks[1], (NUM_EXPERTS, HIDDEN), jnp.float32) * scale, 'router_b': jnp.zeros((NUM_EXPERTS,), jnp.float32), 'up_w': jax.random.normal(ks[2], (NUM_EXPERTS, INTER, HIDDEN), jnp.float32) * scale, 'up_b': jnp.zeros((NUM_EXPERTS, INTER), jnp.float32), 'down_w': jax.random.normal(ks[3], (NUM_EXPERTS, HIDDEN, INTER), jnp.float32) * scale, 'down_b': jnp.zeros((NUM_EXPERTS, HIDDEN), jnp.float32)}
    _L1_ffn_in = _L1_ffn_setup()
    _d = {'L0_attn_x': _L0_attn_in['x'], 'L0_attn_Wq': _L0_attn_in['Wq'], 'L0_attn_bq': _L0_attn_in['bq'], 'L0_attn_Wk': _L0_attn_in['Wk'], 'L0_attn_bk': _L0_attn_in['bk'], 'L0_attn_Wv': _L0_attn_in['Wv'], 'L0_attn_bv': _L0_attn_in['bv'], 'L0_attn_Wo': _L0_attn_in['Wo'], 'L0_attn_bo': _L0_attn_in['bo'], 'L0_ffn_Wr': _L0_ffn_in['Wr'], 'L0_ffn_W1': _L0_ffn_in['W1'], 'L0_ffn_b1': _L0_ffn_in['b1'], 'L0_ffn_W2': _L0_ffn_in['W2'], 'L0_ffn_b2': _L0_ffn_in['b2'], 'L1_attn_Wq': _L1_attn_in['Wq'], 'L1_attn_bq': _L1_attn_in['bq'], 'L1_attn_Wk': _L1_attn_in['Wk'], 'L1_attn_bk': _L1_attn_in['bk'], 'L1_attn_Wv': _L1_attn_in['Wv'], 'L1_attn_bv': _L1_attn_in['bv'], 'L1_attn_Wo': _L1_attn_in['Wo'], 'L1_attn_bo': _L1_attn_in['bo'], 'L1_ffn_ln_scale': _L1_ffn_in['ln_scale'], 'L1_ffn_ln_bias': _L1_ffn_in['ln_bias'], 'L1_ffn_router_w': _L1_ffn_in['router_w'], 'L1_ffn_router_b': _L1_ffn_in['router_b'], 'L1_ffn_up_w': _L1_ffn_in['up_w'], 'L1_ffn_up_b': _L1_ffn_in['up_b'], 'L1_ffn_down_w': _L1_ffn_in['down_w'], 'L1_ffn_down_b': _L1_ffn_in['down_b']}
    _x0 = _d['L0_attn_x']
    _d['L0_attn_x'] = jax.random.normal(jax.random.fold_in(jax.random.key(seed), 1), (8, 256, 128), dtype=_x0.dtype)
    del _x0
    return _d

def reference(L0_attn_x, L0_attn_Wq, L0_attn_bq, L0_attn_Wk, L0_attn_bk, L0_attn_Wv, L0_attn_bv, L0_attn_Wo, L0_attn_bo, L0_ffn_Wr, L0_ffn_W1, L0_ffn_b1, L0_ffn_W2, L0_ffn_b2, L1_attn_Wq, L1_attn_bq, L1_attn_Wk, L1_attn_bk, L1_attn_Wv, L1_attn_bv, L1_attn_Wo, L1_attn_bo, L1_ffn_ln_scale, L1_ffn_ln_bias, L1_ffn_router_w, L1_ffn_router_b, L1_ffn_up_w, L1_ffn_up_b, L1_ffn_down_w, L1_ffn_down_b):

    def _L0_attn_ref(x, Wq, bq, Wk, bk, Wv, bv, Wo, bo):
        import jax, jax.numpy as jnp
        import numpy as np
        EMBED_DIM = 128
        NUM_HEADS = 16
        HEAD_DIM = EMBED_DIM // NUM_HEADS
        B, T, C = x.shape
        H, D = (NUM_HEADS, HEAD_DIM)
        q = (x @ Wq + bq).reshape(B, T, H, D).transpose(0, 2, 1, 3)
        k = (x @ Wk + bk).reshape(B, T, H, D).transpose(0, 2, 1, 3)
        v = (x @ Wv + bv).reshape(B, T, H, D).transpose(0, 2, 1, 3)
        scores = jnp.einsum('bhqd,bhkd->bhqk', q, k) / jnp.sqrt(jnp.float32(D))
        causal = jnp.tril(jnp.ones((T, T), dtype=bool))
        scores = jnp.where(causal, scores, -jnp.inf)
        weights = jax.nn.softmax(scores, axis=-1)
        out = jnp.einsum('bhqk,bhkd->bhqd', weights, v)
        out = out.transpose(0, 2, 1, 3).reshape(B, T, C)
        return out @ Wo + bo

    def _L0_ffn_ref(x, Wr, W1, b1, W2, b2):
        import jax, jax.numpy as jnp
        import numpy as np
        K = 2
        CAP_FACTOR = 1.25
        B, T, C = x.shape
        E = Wr.shape[1]
        capacity = int(T / E * CAP_FACTOR)
        probs = jax.nn.softmax(x @ Wr, axis=-1)
        topk_probs, topk_experts = jax.lax.top_k(probs, K)
        S = T * K
        e_flat = topk_experts.reshape(B, S)
        p_flat = topk_probs.reshape(B, S)
        x_rep = jnp.repeat(x, K, axis=1)
        onehot = jax.nn.one_hot(e_flat, E, dtype=jnp.int32)
        pos_all = jnp.cumsum(onehot, axis=1) - onehot
        pos = jnp.take_along_axis(pos_all, e_flat[..., None], axis=-1)[..., 0]
        keep = pos < capacity
        pos_c = jnp.minimum(pos, capacity - 1)
        b_idx = jnp.broadcast_to(jnp.arange(B)[:, None], (B, S))
        buf = jnp.zeros((E, B, capacity, C), dtype=x.dtype)
        buf = buf.at[e_flat, b_idx, pos_c].add(x_rep * keep[..., None].astype(x.dtype))
        h = jax.nn.relu(jnp.einsum('ebnc,ech->ebnh', buf, W1) + b1[:, None, None, :])
        y = jnp.einsum('ebnh,ehc->ebnc', h, W2) + b2[:, None, None, :]
        y_tok = y[e_flat, b_idx, pos_c]
        y_tok = y_tok * keep[..., None].astype(x.dtype) * p_flat[..., None]
        out = y_tok.reshape(B, T, K, C).sum(axis=2)
        return out

    def _L1_attn_ref(x, Wq, bq, Wk, bk, Wv, bv, Wo, bo):
        import jax, jax.numpy as jnp
        import numpy as np
        DIM, NH, NKV = (128, 16, 4)
        HD = DIM // NH
        B, T = (2, 256)

        def _rotary_freqs(seq_len, dim):
            inv_freq = 1.0 / 10000.0 ** (jnp.arange(0, dim, 2, dtype=jnp.float32) / dim)
            pos = jnp.arange(seq_len, dtype=jnp.float32)
            return pos[:, None] * inv_freq[None, :]

        def _apply_rotary(x, freqs):
            x1, x2 = (x[..., ::2], x[..., 1::2])
            cos, sin = (jnp.cos(freqs), jnp.sin(freqs))
            return jnp.concatenate([x1 * cos - x2 * sin, x1 * sin - x2 * cos], axis=-1)
        Bx, Tx, C = x.shape
        q = (x @ Wq + bq).reshape(Bx, Tx, NH, HD).transpose(0, 2, 1, 3)
        k = (x @ Wk + bk).reshape(Bx, Tx, NKV, HD).transpose(0, 2, 1, 3)
        v = (x @ Wv + bv).reshape(Bx, Tx, NKV, HD).transpose(0, 2, 1, 3)
        freqs = _rotary_freqs(Tx, HD)
        q = _apply_rotary(q, freqs)
        k = _apply_rotary(k, freqs)
        rep = NH // NKV
        k = jnp.repeat(k, rep, axis=1)
        v = jnpp = jnp.repeat(v, rep, axis=1)
        scores = jnp.einsum('bhqd,bhkd->bhqk', q, k) / jnp.sqrt(jnp.float32(HD))
        causal = jnp.tril(jnp.ones((Tx, Tx), dtype=bool))
        scores = jnp.where(causal[None, None], scores, -jnp.inf)
        attn = jax.nn.softmax(scores, axis=-1)
        ctx = jnp.einsum('bhqk,bhkd->bhqd', attn, v)
        out = ctx.transpose(0, 2, 1, 3).reshape(Bx, Tx, C)
        return out @ Wo + bo

    def _L1_ffn_ref(hidden_states, ln_scale, ln_bias, router_w, router_b, up_w, up_b, down_w, down_b):
        import jax, jax.numpy as jnp
        import numpy as np
        HIDDEN = 128
        INTER = 512
        NUM_EXPERTS = 8
        TOP_K = 2
        LN_EPS = 1e-05
        B, S, H = hidden_states.shape
        x = hidden_states.reshape(-1, H)
        mu = jnp.mean(x, axis=-1, keepdims=True)
        var = jnp.var(x, axis=-1, keepdims=True)
        xn = (x - mu) * jax.lax.rsqrt(var + LN_EPS) * ln_scale + ln_bias
        logits = xn @ router_w.T + router_b
        top_w, top_idx = jax.lax.top_k(logits, TOP_K)
        top_w = jax.nn.softmax(top_w.astype(jnp.float32), axis=-1).astype(x.dtype)
        out = jnp.zeros_like(x)
        for e in range(NUM_EXPERTS):
            gate = jnp.sum(jnp.where(top_idx == e, top_w, 0.0), axis=-1)
            h = jax.nn.gelu(x @ up_w[e].T + up_b[e], approximate=False)
            h = h @ down_w[e].T + down_b[e]
            out = out + gate[:, None] * h
        return out.reshape(B, S, H)
    x = L0_attn_x
    xn = _layernorm(x, axis=-1)
    x = x + _L0_attn_ref(xn, L0_attn_Wq, L0_attn_bq, L0_attn_Wk, L0_attn_bk, L0_attn_Wv, L0_attn_bv, L0_attn_Wo, L0_attn_bo) + _L0_ffn_ref(xn, L0_ffn_Wr, L0_ffn_W1, L0_ffn_b1, L0_ffn_W2, L0_ffn_b2)
    xn = _layernorm(x, axis=-1)
    x = x + _L1_attn_ref(xn, L1_attn_Wq, L1_attn_bq, L1_attn_Wk, L1_attn_bk, L1_attn_Wv, L1_attn_bv, L1_attn_Wo, L1_attn_bo) + _L1_ffn_ref(xn, L1_ffn_ln_scale, L1_ffn_ln_bias, L1_ffn_router_w, L1_ffn_router_b, L1_ffn_up_w, L1_ffn_up_b, L1_ffn_down_w, L1_ffn_down_b)
    return x

_drawn_inputs = setup_inputs


def setup_inputs(seed=0):
    import zlib

    import numpy as np

    out = dict(_drawn_inputs(seed))
    spreads = {'L0_attn_bq': (0.0, 0.404),
     'L0_attn_bk': (0.0, 0.8),
     'L0_attn_bv': (0.0, 0.1),
     'L0_attn_bo': (0.0, 0.1),
     'L1_attn_bq': (0.0, 0.8),
     'L1_attn_bk': (0.0, 0.8),
     'L1_attn_bv': (0.0, 0.381),
     'L1_attn_bo': (0.0, 0.1),
     'L1_ffn_ln_scale': (1.0, 0.2),
     'L1_ffn_ln_bias': (0.0, 0.329),
     'L1_ffn_router_b': (0.0, 0.1),
     'L1_ffn_up_b': (0.0, 0.473),
     'L1_ffn_down_b': (0.0, 0.1)}
    factors = {'L0_ffn_Wr': 4.306,
     'L0_ffn_W1': 4.845,
     'L0_ffn_b1': 8.0,
     'L0_ffn_W2': 3.974,
     'L0_ffn_b2': 8.0,
     'L1_attn_Wq': 8.0,
     'L1_attn_Wk': 8.0,
     'L1_attn_Wv': 4.951}
    for name, (base, spread) in spreads.items():
        noise = np.random.default_rng([zlib.crc32(name.encode()), seed]).standard_normal(out[name].shape)
        drawn = base * np.exp(spread * noise) if base else spread * noise
        out[name] = jnp.asarray(drawn.astype(out[name].dtype))
    for name, factor in factors.items():
        out[name] = (out[name] * factor).astype(out[name].dtype)
    return out
```

```python
from contextlib import ExitStack

import numpy as np

import concourse.bass as bass
from concourse import mybir

F32 = mybir.dt.float32
F32R = mybir.dt.float32r
BF16 = mybir.dt.bfloat16
U32 = mybir.dt.uint32
ALU = mybir.AluOpType
ACT = mybir.ActivationFunctionType
AX = mybir.AxisListType

P = 128
NB, T, C = 8, 256, 128
NT = NB * T // P
TPB = T // P
NH, HD = 16, 8
NKV = 4
E0, H0 = 8, 512
CAP = int(T / E0 * 1.25)
NSLOT = E0 * CAP
GCH = [(0, 3), (3, 3), (6, 2)]
E1, H1 = 8, 512
HC = H0 // P
EPS = 1e-5
SCALE = float(HD) ** -0.5
NEG = -1e30
NSTK = 3
NV = 3

CO_ID, CO_MASK, CO_TRI, CO_ONE = 0, P, 2 * P, 3 * P
CO_C, CO_S = 4 * P, 4 * P + T
CO_I8 = 4 * P + 2 * T
CO_IN = CO_I8 + E0
NCONST = CO_IN + CAP


def constants():
    t = np.zeros((P, NCONST), np.float32)
    r, c = np.arange(P)[:, None], np.arange(P)[None, :]
    t[:, CO_ID:CO_ID + P] = r == c
    t[:, CO_MASK:CO_MASK + P] = np.where(c > r, NEG, 0.0)
    t[:, CO_TRI:CO_TRI + P] = r < c
    t[:, CO_ONE:CO_ONE + P] = 1.0
    inv = (np.float32(1.0) / np.float32(10000.0) ** (np.arange(0, HD, 2, dtype=np.float32) / np.float32(HD))).astype(np.float32)
    ang = (np.arange(T, dtype=np.float32)[None, :] * inv[:, None]).astype(np.float32)
    cos, sin = np.cos(ang).astype(np.float32), np.sin(ang).astype(np.float32)
    for row in range(P):
        i = row % HD
        a, b = (cos, sin) if i < HD // 2 else (sin, cos)
        t[row, CO_C:CO_C + T] = a[i % (HD // 2)]
        t[row, CO_S:CO_S + T] = b[i % (HD // 2)]
    t[:, CO_I8:CO_I8 + E0] = np.arange(E0)
    t[:, CO_IN:CO_IN + CAP] = np.arange(1, CAP + 1)
    return t


def attention_plan(L):
    plan = []
    for t in range(NB + 3):
        a, b, c, d = (x if 0 <= x < NB else None for x in (t, t - 1, t - 2, t - 3))

        def add(kind, batch, *rest):
            if batch is not None:
                plan.append((kind, L, batch, *rest))

        if L == 1 and t == 0:
            plan.append(("pre", L, 0))
        if L == 0 and t == 1:
            plan.append(("bias1",))
        add("otr", d)
        for u in range(12):
            add("nat", b, u)
            add("st", c, u // 3, u % 3)
            add("max", b, u)
            add("exp", c, u // 3, u % 3)
            if u % 3 == 2:
                add("msk", c, u // 3)
            if u == 0:
                add("qk", a)
                add("norm", d)
                add("hi", a)
            if u == 1:
                add("lo", a)
                add("stack", a)
                add("ott", d)
            if u == 2:
                add("val", a)
                add("oev", d)
            if u == 3:
                add("vev", a)
                if L == 0 and t == 0:
                    plan += [("route",), ("cum",), ("keys",)]
                add("proj", d)
            if u == 4:
                add("res", d)
                if L == 0:
                    add("disp", a)
            if u == 5:
                add("pv", c, 0)
            if u == 6:
                add("mxt", b, 0)
                add("mrow", b, 0)
                if L == 0:
                    add("dsm", a)
                    add("dse", a)
            if u == 8:
                add("pv", c, 1)
                add("ocp", c, 0)
                if L == 0:
                    add("gt", a, 0)
                    add("gte", a, 0)
            if u == 9 and L == 0:
                add("gt", a, 1)
                add("gte", a, 1)
            if u == 11:
                add("pv", c, 2)
        add("mxt", b, 1)
        add("mrow", b, 1)
        add("pv", c, 3)
        add("ocp", c, 1)
        if L == 1 and t + 1 < NB:
            plan.append(("pre", L, t + 1))
    return plan


def group_heads(g):
    return [8 * (g // 2) + g % 2 + 2 * c for c in range(4)]


def nat_heads(h, v):
    if v < 2:
        return 0, v, group_heads(2 * h + v)
    return 1, v % 2, group_heads(2 * h + v % 2)[2 * (v // 2 - 1):2 * (v // 2)]


def bank_uses(item):
    kind = item[0]
    if kind == "xt":
        return [("N0 N1 S0 S1".split()[item[1] % 4], item)]
    if kind == "lg":
        return [("P0", item)]
    if kind == "cum":
        return [("P1", item)]
    if kind in ("bias", "bias1", "rcon"):
        return [("M0", item)]
    if kind == "nat":
        return [(f"N{item[3] % 2}", item)]
    if kind == "st":
        return [(f"S{(3 * item[3] + item[4]) % 2}", item)]
    if kind == "pv":
        return [(f"P{item[3] // 2}", ("o", item[1], item[2], item[3] // 2))]
    if kind == "otr":
        return [("P0", item + (0,)), ("P1", item + (1,))]
    if kind == "ott":
        return [("P0", item)]
    if kind == "proj":
        return [("P1", item)]
    if kind == "qk":
        return [("M1", item)] if item[1] == 0 else [("M1", item), ("M0", item)]
    if kind == "val":
        return [("M0", item)]
    if kind == "mxt":
        return [("M1", item)]
    if kind == "dsm":
        return [("M0", item)]
    if kind == "gt":
        return [("M1" if item[3] == 0 else "M0", item)]
    if kind == "pre":
        return [("M0", item + (s,)) for s in ("y", "o", "xt", "lg")]
    return []


INPUTS = [
    "L0_attn_x", "L0_attn_Wq", "L0_attn_bq", "L0_attn_Wk", "L0_attn_bk", "L0_attn_Wv", "L0_attn_bv",
    "L0_attn_Wo", "L0_attn_bo", "L0_ffn_Wr", "L0_ffn_W1", "L0_ffn_b1", "L0_ffn_W2", "L0_ffn_b2",
    "L1_attn_Wq", "L1_attn_bq", "L1_attn_Wk", "L1_attn_bk", "L1_attn_Wv", "L1_attn_bv", "L1_attn_Wo",
    "L1_attn_bo", "L1_ffn_ln_scale", "L1_ffn_ln_bias", "L1_ffn_router_w", "L1_ffn_router_b",
    "L1_ffn_up_w", "L1_ffn_up_b", "L1_ffn_down_w", "L1_ffn_down_b"]


def build(nc, w, table, out):
    ctx = ExitStack()
    with ctx:
        def sb(name, shape, dt=F32):
            return ctx.enter_context(nc.sbuf_tensor(name, shape, dt))

        def sem(name):
            return ctx.enter_context(nc.semaphore(name))

        def dram(name, shape):
            return nc.dram_tensor(name, shape, F32, kind="Internal").ap()

        X = sb("X", [P, NT, C])
        XN = sb("XN", [P, NT, C])
        XT = sb("XT", [P, NT * P])
        K = sb("consts", [P, NCONST])
        ident, ones = K[:, CO_ID:CO_ID + P], K[:, CO_ONE:CO_ONE + P]
        cosr, sinr = K[:, CO_C:CO_C + T], K[:, CO_S:CO_S + T]
        identb, maskb, trib, oneb = (sb(n, [P, P], BF16) for n in ("identb", "maskb", "trib", "oneb"))
        Wqkv = [sb(f"Wqkv{L}", [P, 3, C]) for L in range(2)]
        Wo = [sb(f"Wo{L}", [P, C]) for L in range(2)]
        Wr = sb("Wr", [P, E0])
        WqAB = sb("WqAB", [P, 2, C])
        WkAB = sb("WkAB", [P, 2, NKV * HD])
        brow = sb("brow", [1, 4, C])
        browP = sb("browP", [1, 4, C])
        bcol = sb("bcol", [P, 6])
        bvb = [sb(f"bvb{L}", [P, C]) for L in range(2)]
        bob = [sb(f"bob{L}", [P, C]) for L in range(2)]
        b1raw = sb("b1raw", [E0 * HC, P])
        b2raw = sb("b2raw", [E0, C])
        b1T = sb("b1T", [P, E0 * HC])
        b2T = sb("b2T", [P, E0])
        u1raw = sb("u1raw", [E1 * HC, P])
        u1T = sb("u1T", [P, E1 * HC])
        ucol = [sb(f"ucol{i}", [P, HC]) for i in range(2)]
        d2row = sb("d2row", [E1, C])
        lns, lnb = sb("lns", [P, 1]), sb("lnb", [P, 1])
        rwr = sb("rwr", [E1, C])
        rwS, rwB = sb("rwS", [P, E1]), sb("rwB", [P, E1])
        rbb = sb("rbb", [P, E1])
        rc = sb("rc", [P, 2, E1])

        stats = sb("stats", [P, NT, 6])
        mv = sb("mv", [P, NT, 2])
        vpe = sb("vpe", [P, NT])
        rstd = sb("rstd", [P, NT])
        mhalf = sb("mhalf", [P, NT])
        stats2, mv2 = sb("stats2", [P, NT, 6]), sb("mv2", [P, NT, 2])
        rstd2 = sb("rstd2", [P, NT])

        XQ = [sb(f"XQ{i}", [P, 4, T], F32R) for i in range(2)]
        ROT = [sb(f"ROT{i}", [P, 4, T]) for i in range(2)]
        STK = [sb(f"STK{i}", [P, 16, T], F32R) for i in range(NSTK)]
        NM = [sb(f"NM{i}", [P, 2, TPB, NH // 2]) for i in range(2)]
        MS = [sb(f"MS{i}", [NH // 2, 2, T], F32R) for i in range(2)]
        PT = sb("PT", [P, 4, 3, 512])
        VA = [sb(f"VA{i}", [P, TPB, NH, 32]) for i in range(NV)]
        OT = [sb(f"OT{i}", [P, 4 * T]) for i in range(2)]
        rcp = sb("rcp", [P, TPB, NH])
        ON = sb("ON", [P, TPB, C])
        ONT = sb("ONT", [P, T])

        lg = sb("lg", [P, NT, E0])
        top = sb("top", [P, NT, 8])
        tix = sb("tix", [P, NT, 8], U32)
        tif = sb("tif", [P, NT, 2])
        oh = sb("oh", [P, NT, 2, E0])
        sel = sb("sel", [P, NT, E0])
        selb = sb("selb", [P, NT, E0], BF16)
        dlt, ex = sb("dlt", [P, NT, E0]), sb("ex", [P, NT, E0])
        zs, rz = sb("zs", [P, NT]), sb("rz", [P, NT])
        gate = sb("gate", [P, NT, E0])
        key = sb("key", [P, NT, E0])
        DM = sb("DM", [P, TPB, E0, CAP])
        GM = sb("GM", [P, TPB, E0, CAP])
        GT = sb("GT", [P, NB, 3, T])
        xd = sb("xd", [P, NB, E0, CAP])
        ys = sb("ys", [P, 3, P])

        PTf = PT[:, :, :, :].rearrange("p a b c -> p (a b c)")
        F_W = [PTf[:, 1024 * i:1024 * (i + 1)] for i in range(2)]
        F_H = [PTf[:, 2048 + 1280 * i:2048 + 1280 * (i + 1)] for i in range(2)]
        GTf = GT[:, :, :, :].rearrange("p a b c -> p (a b c)")
        XDf = xd[:, :, :, :].rearrange("p a b c -> p (a b c)")
        gT = XDf[0:E1, 0:NT * P]
        D_RAW = [PTf[:, 1024 * i:1024 * (i + 1)] for i in range(2)]
        D_W = [PTf[:, 2048 + 1024 * i:2048 + 1024 * (i + 1)] for i in range(2)]
        D_H = [GTf[:, 2048 * i:2048 * (i + 1)] for i in range(2)]

        names = "N0 N1 S0 S1 P0 P1 M0 M1".split()
        bank = {n: ctx.enter_context(nc.psum_tensor(f"ps_{n}", [P, 512], F32)) for n in names}

        scr = [[dram(f"scr{L}_{b}", (2, P, 4, T)) for b in range(NB)] for L in range(2)]
        scm = [[[dram(f"scm{L}_{b}_{h}", (NH // 2, 2, T)) for h in range(2)] for b in range(NB)] for L in range(2)]

        full = {n: sem(f"full_{n}") for n in names}
        x0_in, x_in, k_in, w_in, wo_in, f_in = (sem(n) for n in ("x0_in", "x_in", "k_in", "w_in", "wo_in", "f_in"))
        const_ok = sem("const_ok")
        va_ok, stk_ok = sem("va_ok"), sem("stk_ok")
        brow_ok = sem("brow_ok")
        bcol_ok = sem("bcol_ok")
        mv_ok, rstd_ok, xn_ok, xt_ok = sem("mv_ok"), sem("rstd_ok"), sem("xn_ok"), sem("xt_ok")
        xbo_ok = sem("xbo_ok")
        dstep = sem("dstep")
        pstep = sem("pstep")
        sel_ok, exin_ok, ex_ok, key_ok, gate_ok, lg_ok, xt0_ok = (
            sem(n) for n in ("sel_ok", "exin_ok", "ex_ok", "key_ok", "gate_ok", "lg_ok", "xt0_ok"))
        qhi_ok, qlo_ok, rot_ok, rsub_ok = sem("qhi_ok"), sem("qlo_ok"), sem("rot_ok"), sem("rsub_ok")
        scr_w = [sem(f"scr_w{i}") for i in range(2)]
        stk_in = [sem(f"stk_in{i}") for i in range(NSTK)]
        val_ok = sem("val_ok")
        nm_ok, mhi_ok, mlo_ok = sem("nm_ok"), sem("mhi_ok"), sem("mlo_ok")
        scm_w = [sem(f"scm_w{i}") for i in range(2)]
        m_in = [[sem(f"m_in{i}{h}") for h in range(2)] for i in range(NSTK)]
        exp_ok, mask_ok, pv_ok = sem("exp_ok"), sem("mask_ok"), sem("pv_ok")
        ocp_ok, on_ok, ont_ok = sem("ocp_ok"), sem("on_ok"), sem("ont_ok")
        dm_ok, gm_ok, gt_ok, xd_ok = (sem(n) for n in ("dm_ok", "gm_ok", "gt_ok", "xd_ok"))
        ab_ok = sem("ab_ok")
        x1_ok = sem("x1_ok")
        fw_in = [sem(f"fw_in{i}") for i in range(2)]
        up_full, up_free, h_ok, y_full, y_ok = (sem(n) for n in ("up_full", "up_free", "h_ok", "y_full", "y_ok"))
        ys_ok, x2_ok, mvb_ok, rstdb_ok, xnb_ok, ybo_ok = (sem(n) for n in ("ys_ok", "x2_ok", "mvb_ok", "rstdb_ok", "xnb_ok", "ybo_ok"))
        lg1_ok = sem("lg1_ok")
        mvc_ok, rstdc_ok, rc_ok, rcin_ok = sem("mvc_ok"), sem("rstdc_ok"), sem("rc_ok"), sem("rcin_ok")
        g1_ok = sem("g1_ok")
        dw_in = [sem(f"dw_in{i}") for i in range(2)]
        wt_full, wt_ok, gu_full, gu_ok, gy_full, gy_free, gT_full, gT_ok, b2_full, b2_ok = (
            sem(n) for n in ("wt_full", "wt_ok", "gu_full", "gu_ok", "gy_full", "gy_free", "gT_full", "gT_ok",
                             "b2_full", "b2_ok"))
        ucol_ok = sem("ucol_ok")
        out_sem = sem("out_sem")

        prologue = [("xt", i) for i in range(4)] + [("lg",), ("bias",)]
        plan0 = attention_plan(0)
        plan1 = [("rcon",)] + attention_plan(1)

        def seq(L, b):
            return L * NB + b

        def released(use):
            kind = use[0]
            if kind == "xt":
                return xt0_ok, use[1] + 1
            if kind in ("lg", "cum", "bias", "bias1", "rcon"):
                return {"lg": (lg_ok, 1), "cum": (key_ok, 1), "bias": (bcol_ok, 1), "bias1": (bcol_ok, 7),
                        "rcon": (rc_ok, 1)}[kind]
            L, b, n = use[1], use[2], seq(use[1], use[2])
            if kind == "nat":
                return nm_ok, 12 * n + use[3] + 1
            if kind == "st":
                return exp_ok, 12 * n + 3 * use[3] + use[4] + 1
            if kind == "o":
                return ocp_ok, 2 * n + use[3] + 1
            if kind == "otr":
                return on_ok, 2 * n + use[3] + 1
            if kind == "qk":
                return (qlo_ok, n + 1) if L == 0 else (rot_ok, b + 1)
            if kind == "mxt":
                return mlo_ok, 2 * n + use[3] + 1
            if kind == "gt":
                return gt_ok, 2 * b + use[3] + 1
            if kind == "pre":
                return {"y": ys_ok, "o": x2_ok, "xt": xt_ok, "lg": lg1_ok}[use[3]], b + 1
            return {"ott": (ont_ok, n + 1), "proj": (x1_ok, n + 1), "val": (val_ok, n + 1), "dsm": (xd_ok, b + 1)}[kind]

        def back(L, b, k):
            n = seq(L, b) - k
            return n // NB, n % NB

        before, filled, last_use, count = {}, {}, {}, dict.fromkeys(names, 0)

        def lay(plan):
            for item in plan:
                for n, use in bank_uses(item):
                    if (n, use) in filled:
                        continue
                    before[n, use] = last_use.get(n)
                    last_use[n] = use
                    if use[0] == "o":
                        filled[n, use] = pv_ok, 4 * seq(use[1], use[2]) + 2 * use[3] + 2
                    else:
                        count[n] += 1
                        filled[n, use] = full[n], count[n]

        lay(prologue + plan0)
        last0 = dict(last_use)
        lay(plan1)

        def await_free(eng, n, use):
            if before[n, use] is not None:
                eng.wait_ge(*released(before[n, use]))

        def await_full(eng, n, use):
            eng.wait_ge(*filled[n, use])

        x_d = w["L0_attn_x"].rearrange("b (q p) c -> p (b q) c", p=P)
        out_d = out.rearrange("b (q p) c -> p (b q) c", p=P)

        def row(name):
            return w[name].rearrange("(a c) -> a c", a=1)

        def down_rows(name, n):
            return row(name).broadcast_to((P, n))

        block = ctx.enter_context(nc.Block())

        @block.sync
        def _(sp):
            sp.dma_start(X[:, 0:4, :], x_d[:, 0:4, :]).then_inc(x0_in, 16)
            sp.dma_start(X[:, 4:NT, :], x_d[:, 4:NT, :]).then_inc(x_in, 16)
            sp.dma_start(K[:], table).then_inc(k_in, 16)
            sp.dma_start(Wr[:], w["L0_ffn_Wr"]).then_inc(w_in, 16)
            sp.dma_start(Wqkv[0][:, 0, :], w["L0_attn_Wq"]).then_inc(w_in, 16)
            sp.dma_start(Wqkv[0][:, 1, :], w["L0_attn_Wk"]).then_inc(w_in, 16)
            sp.dma_start(Wqkv[0][:, 2, :], w["L0_attn_Wv"]).then_inc(w_in, 16)

            def stack(L, b):
                n, i, s = seq(L, b), b % 2, b % NSTK
                rows = P if L == 0 else NKV * HD
                xq = XQ[i][:].bitcast(F32)
                sp.wait_ge(qlo_ok, n + 1)
                for part in range(2):
                    sp.dma_start(scr[L][b][0][:, 2 * part:2 * part + 2, :],
                                 xq[:, part:part + 1, :].broadcast_to((P, 2, T))).then_inc(scr_w[i], 16)
                sp.dma_start(scr[L][b][1][0:rows].rearrange("r (e s) t -> r e (s t)", e=2),
                             xq[0:rows, 2:4, :].rearrange("r s t -> r (s t)")[:, None, :]
                             .broadcast_to((rows, 2, 2 * T))).then_inc(scr_w[i], 16)
                sp.wait_ge(scr_w[i], 48 * (n // 2 + 1))
                if b >= NSTK or L == 1:
                    old = (L, b - NSTK) if b >= NSTK else (0, NB - 1)
                    await_full(sp, "S1", ("st", *old, 3, 2))
                else:
                    sp.wait_ge(stk_ok, 2 * NSTK)
                stk = STK[s][:].bitcast(F32)
                for p in range(2):
                    if L == 0:
                        sp.dma_start(stk[64 * p:64 * p + 32, :, :],
                                     scr[L][b].rearrange("k (j p d) s t -> p (d s) (k j) t", p=2, d=HD)[p])\
                          .then_inc(stk_in[s], 16)
                    else:
                        sp.dma_start(stk[64 * p:64 * p + 32, 0:8, :],
                                     scr[L][b][0].rearrange("(j p d) s t -> p (d s) j t", p=2, d=HD)[p])\
                          .then_inc(stk_in[s], 16)
                        sp.dma_start(stk[64 * p:64 * p + 32, 8:8 + NKV, :],
                                     scr[L][b][1][0:rows].rearrange("(j d) s t -> (d s) j t", d=HD))\
                          .then_inc(stk_in[s], 16)

            def mrow(L, b, h):
                n = 2 * seq(L, b) + h
                sp.wait_ge(mlo_ok, n + 1)
                sp.dma_start(scm[L][b][h], MS[h][:].bitcast(F32)).then_inc(scm_w[h], 16)
                sp.wait_ge(scm_w[h], 16 * (seq(L, b) + 1))
                for p in range(2):
                    sp.dma_start(STK[b % NSTK][64 * p + 32:64 * p + 34, 4 * h:4 * h + 4, :].bitcast(F32),
                                 scm[L][b][h].rearrange("(j p) s t -> p s j t", p=2)[p])\
                      .then_inc(m_in[b % NSTK][h], 16)

            def attention(plan):
                for item in plan:
                    if item[0] == "stack":
                        stack(*item[1:])
                    if item[0] == "mrow":
                        mrow(*item[1:])

            attention(plan0)
            sp.wait_ge(ocp_ok, 2 * NB)
            sp.wait_ge(mask_ok, 4 * NB)
            sp.wait_ge(pv_ok, 4 * NB)
            for e in range(2):
                sp.dma_start(F_W[e][:, 0:H0], w["L0_ffn_W1"][e]).then_inc(fw_in[e], 16)
                sp.dma_start(F_W[e][:, H0:].rearrange("p (m c) -> p m c", m=HC),
                             w["L0_ffn_W2"][e].rearrange("(m p) c -> p m c", p=P)).then_inc(fw_in[e], 16)
            with sp.Fori(2, E0 - 1, 2) as e0:
                for i in range(2):
                    sp.wait_ge(y_full, e0 + (i - 1))
                    sp.dma_start(F_W[i][:, 0:H0], w["L0_ffn_W1"][bass.ds(e0 + i, 1)].rearrange("a p n -> (a p) n"))\
                      .then_inc(fw_in[i], 16)
                    sp.dma_start(F_W[i][:, H0:].rearrange("p (m c) -> p m c", m=HC),
                                 w["L0_ffn_W2"][bass.ds(e0 + i, 1)].rearrange("a (m p) c -> p (a m) c", p=P))\
                      .then_inc(fw_in[i], 16)
            attention(plan1)

            def expert_raw(e, i, many):
                up = w["L1_ffn_up_w"][bass.ds(e, 1)].rearrange("a (m p) c -> p (a m) c", p=P) if many else \
                    w["L1_ffn_up_w"][e].rearrange("(m p) c -> p m c", p=P)
                dn = w["L1_ffn_down_w"][bass.ds(e, 1)].rearrange("a p n -> (a p) n") if many else \
                    w["L1_ffn_down_w"][e]
                sp.dma_start(D_RAW[i][:, 0:H1].rearrange("p (m c) -> p m c", m=HC), up).then_inc(dw_in[i], 16)
                sp.dma_start(D_RAW[i][:, H1:], dn).then_inc(dw_in[i], 16)

            sp.wait_ge(pv_ok, 8 * NB)
            sp.wait_ge(mask_ok, 8 * NB)
            for e in range(2):
                expert_raw(e, e, False)
            with sp.Fori(2, E1 - 1, 2) as e0:
                for i in range(2):
                    sp.wait_ge(wt_full, 2 * (e0 + (i - 1)))
                    expert_raw(e0 + i, i, True)
            sp.wait_ge(gy_free, E1 * 4 + 2)
            sp.dma_start(out_d, X[:]).then_inc(out_sem, 16)
            sp.wait_ge(out_sem, 16)

        @block.gpsimd
        def _(pool):
            pool.memset(mhalf[:], -0.5).then_inc(pstep, 1)
            pool.wait_ge(pstep, 1)
            for i in range(NSTK):
                for p in range(2):
                    pool.memset(STK[i][64 * p + 32:64 * p + 34, 8:16, :].bitcast(F32), 1.0).then_inc(stk_ok, 1)
                    pool.wait_ge(stk_ok, 2 * i + p + 1)
            def load_wo(L, sem):
                for g in range(4):
                    src = w[f"L{L}_attn_Wo"].rearrange("(h c p d) n -> h p c d n", h=2, p=2, d=HD)[g // 2, g % 2]
                    pool.dma_start(Wo[L][32 * g:32 * g + 32, :], src).then_inc(sem, 16)

            names_rows = ["L0_attn_bq", "L0_attn_bk", "L1_attn_bq"]
            for i, n in enumerate(names_rows):
                pool.dma_start(brow[0:1, i, :], row(n)).then_inc(brow_ok, 16)
            pool.dma_start(brow[0:1, 3, 0:NKV * HD], row("L1_attn_bk")).then_inc(brow_ok, 16)
            pool.dma_start(bvb[0][:], down_rows("L0_attn_bv", C)).then_inc(wo_in, 16)
            load_wo(0, wo_in)
            pool.dma_start(bob[0][:], down_rows("L0_attn_bo", C)).then_inc(wo_in, 16)
            pool.dma_start(b1raw[:], w["L0_ffn_b1"].rearrange("e (m p) -> (e m) p", p=P)).then_inc(f_in, 16)
            pool.dma_start(b2raw[:], w["L0_ffn_b2"]).then_inc(f_in, 16)
            pool.dma_start(u1raw[:], w["L1_ffn_up_b"].rearrange("e (m p) -> (e m) p", p=P)).then_inc(f_in, 16)
            pool.dma_start(d2row[:], w["L1_ffn_down_b"]).then_inc(f_in, 16)
            pool.dma_start(rwr[:], w["L1_ffn_router_w"]).then_inc(f_in, 16)
            pool.dma_start(Wqkv[1][:, 0, :], w["L1_attn_Wq"]).then_inc(f_in, 16)
            pool.dma_start(Wqkv[1][:, 1, 0:NKV * HD], w["L1_attn_Wk"]).then_inc(f_in, 16)
            pool.dma_start(Wqkv[1][:, 2, 0:NKV * HD], w["L1_attn_Wv"]).then_inc(f_in, 16)
            load_wo(1, f_in)
            pool.dma_start(bvb[1][:, 0:NKV * HD], down_rows("L1_attn_bv", NKV * HD)).then_inc(f_in, 16)
            pool.dma_start(bob[1][:], down_rows("L1_attn_bo", C)).then_inc(f_in, 16)
            pool.dma_start(rbb[:], down_rows("L1_ffn_router_b", E1)).then_inc(f_in, 16)
            pool.dma_start(lns[:], w["L1_ffn_ln_scale"].rearrange("(c a) -> c a", a=1)).then_inc(f_in, 16)
            pool.dma_start(lnb[:], w["L1_ffn_ln_bias"].rearrange("(c a) -> c a", a=1)).then_inc(f_in, 16)
            for i in range(NV):
                pool.memset(VA[i][:], 0.0).then_inc(pstep, 1)
            pool.wait_ge(pstep, 1 + NV)
            for i in range(NV):
                pool.memset(VA[i][:, :, :, HD:HD + 1], 1.0).then_inc(va_ok, 1)

            pool.wait_ge(mv_ok, 1)
            pool.tensor_scalar(vpe[:], mv[:, :, 1], EPS, 1.0, ALU.add, ALU.mult).then_inc(pstep, 1)
            pool.wait_ge(pstep, 2 + NV)
            pool.tensor_tensor(rstd[:], vpe[:], mhalf[:], ALU.pow).then_inc(rstd_ok, 1)
            pool.wait_ge(xn_ok, NT)
            pool.wait_ge(wo_in, 16 * 6)
            pool.tensor_tensor(X[:], X[:], bob[0][:, None, :].broadcast_to((P, NT, C)), ALU.add).then_inc(xbo_ok, 1)

            def split_columns():
                pool.wait_ge(f_in, 16 * 17)
                pool.wait_ge(brow_ok, 64)
                for a in range(2):
                    pool.tensor_copy(WqAB[:, a, :].rearrange("c (h r i) -> c h r i", r=2, i=4),
                                     Wqkv[1][:, 0, :].rearrange("c (h i a) -> c h i a", i=4, a=2)[:, :, None, :, a]
                                     .broadcast_to((P, NH, 2, 4)))
                    pool.tensor_copy(WkAB[:, a, :].rearrange("c (h r i) -> c h r i", r=2, i=4),
                                     Wqkv[1][:, 1, 0:NKV * HD].rearrange("c (h i a) -> c h i a", i=4, a=2)[:, :, None, :, a]
                                     .broadcast_to((P, NKV, 2, 4)))
                    pool.tensor_copy(browP[0:1, a, :].rearrange("c (h r i) -> c h r i", r=2, i=4),
                                     brow[0:1, 2, :].rearrange("c (h i a) -> c h i a", i=4, a=2)[:, :, None, :, a]
                                     .broadcast_to((1, NH, 2, 4)))
                    last = pool.tensor_copy(browP[0:1, 2 + a, 0:NKV * HD].rearrange("c (h r i) -> c h r i", r=2, i=4),
                                            brow[0:1, 3, 0:NKV * HD].rearrange("c (h i a) -> c h i a", i=4, a=2)[:, :, None, :, a]
                                            .broadcast_to((1, NKV, 2, 4)))
                last.then_inc(ab_ok, 1)

            def mask(L, b, g):
                n = 4 * seq(L, b) + g
                pool.wait_ge(exp_ok, 3 * (n + 1))
                diag = [PT[:, g, 0:2, :].rearrange("k r (i q) -> k (r i) q", i=2)[:, :, 0:P],
                        PT[:, g, 2, :].rearrange("k (i q) -> k i q", i=4)]
                for v in diag:
                    last = pool.affine_select(out=v, in_=v, compare_op=ALU.is_ge, fill=0.0, base=0,
                                              pattern=[[0, 4], [1, P]], channel_multiplier=-1)
                last.then_inc(mask_ok, 1)

            def gated(b):
                if b > 0:
                    await_full(pool, "M0", ("gt", 0, b - 1, 1))
                pool.wait_ge(dm_ok, b + 1)
                pool.wait_ge(gate_ok, 1)
                pool.tensor_tensor(GM[:], DM[:], gate[:, 2 * b:2 * b + 2, :, None].broadcast_to((P, TPB, E0, CAP)),
                                   ALU.mult).then_inc(gm_ok, 1)

            def norm1(b):
                s = slice(2 * b, 2 * b + 2)
                pool.wait_ge(mvb_ok, b + 1)
                pool.tensor_scalar(vpe[:, s], mv[:, s, 1], EPS, 1.0, ALU.add, ALU.mult).then_inc(pstep, 1)
                pool.wait_ge(pstep, 3 + NV + 2 * b)
                pool.tensor_tensor(rstd[:, s], vpe[:, s], mhalf[:, s], ALU.pow).then_inc(rstdb_ok, 1)
                pool.wait_ge(xnb_ok, 2 * (b + 1))
                pool.tensor_tensor(X[:, s, :], X[:, s, :], bob[1][:, None, :].broadcast_to((P, TPB, C)), ALU.add)\
                    .then_inc(ybo_ok, 1)
                pool.wait_ge(mvc_ok, b + 1)
                pool.tensor_scalar(vpe[:, s], mv2[:, s, 1], EPS, 1.0, ALU.add, ALU.mult).then_inc(pstep, 1)
                pool.wait_ge(pstep, 4 + NV + 2 * b)
                pool.tensor_tensor(rstd2[:, s], vpe[:, s], mhalf[:, s], ALU.pow).then_inc(rstdc_ok, 1)

            def rotate(b):
                n, i = b, b % 2
                pool.wait_ge(rot_ok, n + 1)
                for j, rows in ((0, P), (2, NKV * HD)):
                    last = pool.tensor_tensor(ROT[i][0:rows, j, :], ROT[i][0:rows, j, :], ROT[i][0:rows, j + 1, :],
                                              ALU.subtract)
                last.then_inc(rsub_ok, 1)

            for item in plan0:
                if item[0] == "msk":
                    mask(*item[1:])
                if item[0] == "disp":
                    gated(item[2])
                if item[0] == "bias1":
                    split_columns()
            for item in plan1:
                if item[0] == "msk":
                    mask(*item[1:])
                if item[0] == "pre":
                    norm1(item[2])
                if item[0] == "qk":
                    rotate(item[2])

        @block.scalar
        def _(act):
            act.wait_ge(k_in, 16)
            for i in range(4):
                n = f"{'NNSS'[i]}{i % 2}"
                await_full(act, n, ("xt", i))
                act.activation(XT[:, 512 * i:512 * (i + 1)], bank[n][:], ACT.Copy).then_inc(xt0_ok, 1)
            await_full(act, "M0", ("bias",))
            act.activation(bcol[:, 0:2], bank["M0"][:, 0:2], ACT.Copy).then_inc(bcol_ok, 1)

            def bias1():
                await_full(act, "M0", ("bias1",))
                act.activation(bcol[:, 2:6], bank["M0"][:, 2:6], ACT.Copy).then_inc(bcol_ok, 1)
                act.activation(b1T[:], bank["M0"][:, 32:64], ACT.Copy).then_inc(bcol_ok, 1)
                act.activation(u1T[:], bank["M0"][:, 64:96], ACT.Copy).then_inc(bcol_ok, 1)
                act.activation(b2T[:], bank["M0"][:, 96:104], ACT.Copy).then_inc(bcol_ok, 1)
                act.activation(rwS[:], bank["M0"][:, 104:112], ACT.Copy).then_inc(bcol_ok, 1)
                act.activation(rwB[:], bank["M0"][:, 104:112], ACT.Copy).then_inc(bcol_ok, 1)

            def route():
                act.wait_ge(exin_ok, 1)
                act.activation(ex[:], dlt[:], ACT.Exp).then_inc(ex_ok, 1)

            def high(L, b):
                n, i = seq(L, b), b % 2
                if n >= 2:
                    act.wait_ge(scr_w[i], 48 * (n // 2))
                if L == 0:
                    act.wait_ge(bcol_ok, 1)
                    await_full(act, "M1", ("qk", L, b))
                    act.activation(XQ[i][:, 0, :], bank["M1"][:, 0:T], ACT.Identity, bias=bcol[:, 0:1])
                    act.activation(XQ[i][:, 2, :], bank["M1"][:, T:2 * T], ACT.Identity, bias=bcol[:, 1:2])\
                        .then_inc(qhi_ok, 1)
                else:
                    act.wait_ge(rsub_ok, b + 1)
                    act.activation(XQ[i][:, 0, :], ROT[i][:, 0, :], ACT.Copy)
                    act.activation(XQ[i][0:32, 2, :], ROT[i][0:32, 2, :], ACT.Copy).then_inc(qhi_ok, 1)

            def exps(L, b, g, r):
                n, u = 4 * seq(L, b) + g, 3 * g + r
                s = f"S{u % 2}"
                if r == 0 and n >= 4:
                    act.wait_ge(pv_ok, n - 3)
                await_full(act, s, ("st", L, b, g, r))
                act.activation(PT[:, g, r, :], bank[s][:], ACT.Exp, scale=SCALE).then_inc(exp_ok, 1)

            def max_high(L, b, h):
                n = 2 * seq(L, b) + h
                if n >= 2:
                    act.wait_ge(scm_w[h], 16 * seq(L, b))
                await_full(act, "M1", ("mxt", L, b, h))
                act.activation(MS[h][:, 0, :], bank["M1"][0:NH // 2, 0:T], ACT.Copy).then_inc(mhi_ok, 1)

            def copy_o(L, b, h):
                n = seq(L, b)
                if n >= 2 and h == 0:
                    await_full(act, "P1", ("otr", *back(L, b, 2), 1))
                p = f"P{h}"
                await_full(act, p, ("o", L, b, h))
                act.activation(OT[b % 2][:, 512 * h:512 * (h + 1)], bank[p][:], ACT.Copy).then_inc(ocp_ok, 1)

            def copy_ont(L, b):
                n = seq(L, b)
                await_full(act, "P0", ("ott", L, b))
                if n >= 1:
                    await_full(act, "P1", ("proj", *back(L, b, 1)))
                act.activation(ONT[:], bank["P0"][:, 0:T], ACT.Copy).then_inc(ont_ok, 1)

            def copy_xd(b):
                await_full(act, "M0", ("dsm", 0, b))
                act.activation(xd[:, b, :, :].rearrange("c e n -> c (e n)"), bank["M0"][:, 0:NSLOT], ACT.Copy)\
                    .then_inc(xd_ok, 1)

            def copy_gt(b, k):
                if k == 0:
                    await_full(act, "M1", ("gt", 0, b, 0))
                    n = GCH[0][1] * CAP
                    act.activation(GT[0:n, b, 0:2, :], bank["M1"][0:n, :].rearrange("n (k q) -> n k q", k=2), ACT.Copy)\
                        .then_inc(gt_ok, 1)
                else:
                    await_full(act, "M0", ("gt", 0, b, 1))
                    n = GCH[2][1] * CAP
                    act.activation(GT[0:n, b, 2, :], bank["M0"][0:n, 0:T], ACT.Copy)\
                        .then_inc(gt_ok, 1)

            def pre(b):
                await_full(act, "M0", ("pre", 1, b, "y"))
                if b >= 1:
                    await_full(act, "M0", ("pre", 1, b - 1, "o"))
                for j, (_, ne) in ((0, GCH[0]), (2, GCH[2])):
                    n, k = ne * CAP, 2 if j == 0 else 1
                    last = act.activation(ys[0:n, j:j + k, :],
                                          bank["M0"][0:n, P * j:P * (j + k)].rearrange("n (k c) -> n k c", k=k), ACT.Copy)
                last.then_inc(ys_ok, 1)
                await_full(act, "M0", ("pre", 1, b, "xt"))
                act.activation(XT[:, T * b:T * (b + 1)], bank["M0"][:, 0:T], ACT.Copy).then_inc(xt_ok, 1)

            def attention(plan):
                for item in plan:
                    k = item[0]
                    if k == "hi":
                        high(*item[1:])
                    if k == "exp":
                        exps(*item[1:])
                    if k == "mrow":
                        max_high(*item[1:])
                    if k == "ocp":
                        copy_o(*item[1:])
                    if k == "oev":
                        copy_ont(*item[1:])
                    if k == "dse":
                        copy_xd(item[2])
                    if k == "gte":
                        copy_gt(*item[2:])
                    if k == "pre":
                        pre(item[2])
                    if k == "bias1":
                        bias1()
                    if k == "route":
                        route()

            attention(plan0)
            act.wait_ge(bcol_ok, 7)
            with act.Fori(0, E0 - 1, 2) as e0:
                for i in range(2):
                    act.activation(ucol[i][:], b1T[:, bass.ds((e0 + i) * HC, HC)], ACT.Copy).then_inc(ucol_ok, 1)
                    act.wait_ge(ucol_ok, e0 + (i + 1))
                    for m in range(HC):
                        act.wait_ge(up_full, HC * (e0 + i) + (m + 1))
                        act.activation(F_H[i][:, NSLOT * m:NSLOT * (m + 1)],
                                       bank[f"{'NS'[m // 2]}{m % 2}"][:, 0:NSLOT], ACT.Relu,
                                       bias=ucol[i][:, m:m + 1]).then_inc(h_ok, 1)
            attention(plan1)
            act.wait_ge(exin_ok, 2)
            act.activation(top[:, :, 2:4], tif[:], ACT.Exp).then_inc(ex_ok, 1)
            for g in range(4):
                act.wait_ge(gT_full, g + 1)
                act.activation(gT[:, 512 * g:512 * (g + 1)], bank[f"N{g % 2}"][0:E1, :], ACT.Copy).then_inc(gT_ok, 1)
            act.sem_inc(gu_ok, 4)
            with act.Fori(0, E1 - 1, 2) as e0:
                for i in range(2):
                    act.activation(ucol[i][:], u1T[:, bass.ds((e0 + i) * HC, HC)], ACT.Copy).then_inc(ucol_ok, 1)
                    act.wait_ge(ucol_ok, e0 + (E0 + i + 1))
                    for tc in range(4):
                        for m in range(HC):
                            act.wait_ge(gu_full, 16 * (e0 + i) + (4 * tc + m + 1))
                            act.activation(D_H[tc % 2][:, 512 * m:512 * (m + 1)], bank[f"{'NS'[m // 2]}{m % 2}"][:],
                                           ACT.Gelu, bias=ucol[i][:, m:m + 1]).then_inc(gu_ok, 1)

        @block.vector
        def _(dve):
            chain = [0]

            def link(ins):
                chain[0] += 1
                ins.then_inc(dstep, 1)
                dve.wait_ge(dstep, chain[0])

            dve.wait_ge(x0_in, 16)
            for i in range(NT):
                if i == 4:
                    dve.wait_ge(x_in, 16)
                last = dve.bn_stats(stats[:, i, :], X[:, i, :])
            link(last)
            for i in range(NT):
                last = dve.bn_aggr(mv[:, i, :], stats[:, i, :])
            last.then_inc(mv_ok, 1)
            dve.wait_ge(mv_ok, 1)
            dve.wait_ge(k_in, 16)
            for dst, at in ((identb, CO_ID), (maskb, CO_MASK), (trib, CO_TRI), (oneb, CO_ONE)):
                last = dve.tensor_copy(dst[:], K[:, at:at + P])
            last.then_inc(const_ok, 1)
            dve.wait_ge(rstd_ok, 1)
            for i in range(NT):
                dve.tensor_scalar(XN[:, i, :], X[:, i, :], mv[:, i, 0:1], rstd[:, i:i + 1], ALU.subtract, ALU.mult)\
                    .then_inc(xn_ok, 1)

            def top2():
                for i in range(NT):
                    last = dve.max(top[:, i, :], lg[:, i, :])
                link(last)
                for i in range(NT):
                    last = dve.max_index(tix[:, i, :], top[:, i, :], lg[:, i, :])
                link(last)
                link(dve.tensor_copy(tif[:], tix[:, :, 0:2]))
                for k in range(2):
                    last = dve.tensor_tensor(oh[:, :, k, :], K[:, None, CO_I8:CO_I8 + E0].broadcast_to((P, NT, E0)),
                                             tif[:, :, k:k + 1].broadcast_to((P, NT, E0)), ALU.is_equal)
                link(last)

            def route():
                await_full(dve, "P0", ("lg",))
                dve.tensor_copy(lg[:].rearrange("p a e -> p (a e)"), bank["P0"][:, 0:NT * E0]).then_inc(lg_ok, 1)
                dve.wait_ge(lg_ok, 1)
                top2()
                link(dve.tensor_tensor(sel[:], oh[:, :, 0, :], oh[:, :, 1, :], ALU.add))
                dve.tensor_copy(selb[:], sel[:]).then_inc(sel_ok, 1)
                dve.tensor_tensor(dlt[:], lg[:], top[:, :, 0:1].broadcast_to((P, NT, E0)), ALU.subtract)\
                    .then_inc(exin_ok, 1)
                dve.wait_ge(ex_ok, 1)
                link(dve.tensor_reduce(zs[:], ex[:], AX.X, ALU.add))
                link(dve.reciprocal(rz[:], zs[:]))
                dve.tensor_tensor(gate[:], ex[:], rz[:, :, None].broadcast_to((P, NT, E0)), ALU.mult).then_inc(gate_ok, 1)

            def keys():
                await_full(dve, "P1", ("cum",))
                dve.scalar_tensor_tensor(out=key[:].rearrange("p a e -> p (a e)"), in0=bank["P1"][:, 0:NT * E0],
                                         scalar=1.0, in1=sel[:].rearrange("p a e -> p (a e)"),
                                         op0=ALU.add, op1=ALU.mult).then_inc(key_ok, 1)
                dve.wait_ge(key_ok, 1)

            def row_max(L, b, u):
                n = seq(L, b)
                if u == 0 and n >= 2:
                    await_full(dve, "M1", ("mxt", *back(L, b, 2), 1))
                h, v = u // 6, u % 6
                qt, p, heads = nat_heads(h, v)
                many, first = len(heads), heads[0] // 2 % 4
                s = f"N{u % 2}"
                await_full(dve, s, ("nat", L, b, u))
                dve.tensor_reduce(NM[b % 2][:, h, qt, :].rearrange("q (j p) -> q p j", p=2)[:, p, first:first + many],
                                  bank[s][:].rearrange("q (h k) -> q h k", h=many), AX.X, ALU.max, negate=True)\
                    .then_inc(nm_ok, 1)

            def low(L, b):
                n, i = seq(L, b), b % 2
                dve.wait_ge(qhi_ok, n + 1)
                if L == 0:
                    for j in range(2):
                        last = dve.scalar_tensor_tensor(out=XQ[i][:, 2 * j + 1, :], in0=bank["M1"][:, j * T:(j + 1) * T],
                                                        scalar=bcol[:, j:j + 1], in1=XQ[i][:, 2 * j, :].bitcast(F32),
                                                        op0=ALU.add, op1=ALU.subtract)
                    last.then_inc(qlo_ok, 1)
                else:
                    for j, rows in ((0, P), (2, NKV * HD)):
                        last = dve.tensor_tensor(XQ[i][0:rows, j + 1, :], ROT[i][0:rows, j, :],
                                                 XQ[i][0:rows, j, :].bitcast(F32), ALU.subtract)
                    last.then_inc(qlo_ok, 1)

            def rotary(b):
                i = b % 2
                if b >= 2:
                    dve.wait_ge(qlo_ok, NB + b - 1)
                dve.wait_ge(rc_ok, 1)
                for j, (n, rows, col) in enumerate((("M1", P, 2), ("M0", NKV * HD, 4))):
                    await_full(dve, n, ("qk", 1, b))
                    for a, tab in ((0, cosr), (1, sinr)):
                        last = dve.scalar_tensor_tensor(out=ROT[i][0:rows, 2 * j + a, :],
                                                        in0=bank[n][0:rows, a * T:(a + 1) * T],
                                                        scalar=bcol[0:rows, col + a:col + a + 1], in1=tab[0:rows, :],
                                                        op0=ALU.add, op1=ALU.mult)
                last.then_inc(rot_ok, 1)

            def values(L, b):
                n = seq(L, b)
                nk = NH if L == 0 else NKV
                await_full(dve, "M0", ("val", L, b))
                if n == 0:
                    dve.wait_ge(va_ok, NV)
                    dve.wait_ge(wo_in, 16 * 6)
                if n >= NV:
                    dve.wait_ge(pv_ok, 4 * (n - NV + 1) if b >= NV else 4 * NB)
                dve.tensor_tensor(VA[b % NV][:, :, 0:nk, 0:HD],
                                  bank["M0"][:, 0:TPB * nk * HD].rearrange("k (t h d) -> k t h d", t=TPB, h=nk),
                                  bvb[L][:, 0:nk * HD].rearrange("k (h d) -> k h d", h=nk)[:, None, :, :]
                                  .broadcast_to((P, TPB, nk, HD)), ALU.add).then_inc(val_ok, 1)

            def max_low(L, b, h):
                n = 2 * seq(L, b) + h
                dve.wait_ge(mhi_ok, n + 1)
                dve.tensor_tensor(MS[h][:, 1, :], bank["M1"][0:NH // 2, 0:T], MS[h][:, 0, :].bitcast(F32), ALU.subtract)\
                    .then_inc(mlo_ok, 1)

            def normalise(L, b):
                n = seq(L, b)
                for q in range(TPB):
                    await_full(dve, f"P{q}", ("otr", L, b, q))
                    o = bank[f"P{q}"][:].rearrange("q (h w) -> q h w", w=32)
                    link(dve.reciprocal(rcp[:, q, :, None], o[:, :, HD:HD + 1]))
                    if n >= 1 and q == 0:
                        await_full(dve, "P0", ("ott", *back(L, b, 1)))
                    dve.tensor_tensor(ON[:, q, :].rearrange("q (h d) -> q h d", h=NH), o[:, :, 0:HD],
                                      rcp[:, q, :, None].broadcast_to((P, NH, HD)), ALU.mult).then_inc(on_ok, 1)

            def residual(L, b):
                n = seq(L, b)
                await_full(dve, "P1", ("proj", L, b))
                if L == 0:
                    dve.wait_ge(xbo_ok, 1)
                else:
                    dve.wait_ge(ybo_ok, b + 1)
                dve.tensor_tensor(X[:, 2 * b:2 * b + 2, :], bank["P1"][:, 0:T].rearrange("q (t c) -> q t c", t=2),
                                  X[:, 2 * b:2 * b + 2, :], ALU.add).then_inc(x1_ok, 1)

            def dispatch(b):
                if b > 0:
                    await_full(dve, "M0", ("dsm", 0, b - 1))
                    dve.wait_ge(gm_ok, b)
                for q in range(TPB):
                    last = dve.tensor_tensor(DM[:, q, :, :], K[:, None, CO_IN:CO_IN + CAP].broadcast_to((P, E0, CAP)),
                                             key[:, 2 * b + q, :, None].broadcast_to((P, E0, CAP)), ALU.is_equal)
                last.then_inc(dm_ok, 1)

            def router_constants():
                dve.wait_ge(f_in, 16 * 17)
                dve.tensor_scalar(rwS[:], rwS[:], lns[:, 0:1], None, ALU.mult).then_inc(rcin_ok, 1)
                dve.tensor_scalar(rwB[:], rwB[:], lnb[:, 0:1], None, ALU.mult).then_inc(rcin_ok, 1)
                await_full(dve, "M0", ("rcon",))
                dve.tensor_copy(rc[:, 0, :], bank["M0"][:, 0:E1])
                dve.tensor_tensor(rc[:, 1, :], bank["M0"][:, E1:2 * E1], rbb[:], ALU.add).then_inc(rc_ok, 1)

            def pre(b):
                s = slice(2 * b, 2 * b + 2)
                await_full(dve, "M0", ("pre", 1, b, "o"))
                dve.wait_ge(x1_ok, b + 1)
                dve.tensor_tensor(X[:, s, :], bank["M0"][:, 0:T].rearrange("q (t c) -> q t c", t=2), X[:, s, :], ALU.add)\
                    .then_inc(x2_ok, 1)
                dve.wait_ge(x2_ok, b + 1)
                for i in (2 * b, 2 * b + 1):
                    last = dve.bn_stats(stats[:, i, :], X[:, i, :])
                link(last)
                for i in (2 * b, 2 * b + 1):
                    last = dve.bn_aggr(mv[:, i, :], stats[:, i, :])
                last.then_inc(mvb_ok, 1)
                dve.wait_ge(mvb_ok, b + 1)
                dve.wait_ge(rstdb_ok, b + 1)
                for i in (2 * b, 2 * b + 1):
                    dve.tensor_scalar(XN[:, i, :], X[:, i, :], mv[:, i, 0:1], rstd[:, i:i + 1], ALU.subtract, ALU.mult)\
                        .then_inc(xnb_ok, 1)
                dve.wait_ge(xnb_ok, 2 * b + 2)
                for i in (2 * b, 2 * b + 1):
                    last = dve.bn_stats(stats2[:, i, :], XN[:, i, :])
                link(last)
                for i in (2 * b, 2 * b + 1):
                    last = dve.bn_aggr(mv2[:, i, :], stats2[:, i, :])
                last.then_inc(mvc_ok, 1)
                await_full(dve, "M0", ("pre", 1, b, "lg"))
                dve.tensor_copy(lg[:, s, :].rearrange("p a e -> p (a e)"), bank["M0"][:, 0:2 * E1]).then_inc(lg1_ok, 1)

            def route1():
                dve.wait_ge(rstdc_ok, NB)
                dve.wait_ge(mvc_ok, NB)
                dve.wait_ge(rc_ok, 1)
                dve.wait_ge(lg1_ok, NB)

                def bc(x):
                    return x.broadcast_to((P, NT, E1))
                link(dve.tensor_tensor(dlt[:], bc(mv2[:, :, 0:1]), bc(rc[:, 0:1, :]), ALU.mult))
                link(dve.tensor_tensor(ex[:], lg[:], dlt[:], ALU.subtract))
                link(dve.tensor_tensor(dlt[:], ex[:], bc(rstd2[:, :, None]), ALU.mult))
                link(dve.tensor_tensor(lg[:], dlt[:], bc(rc[:, 1:2, :]), ALU.add))
                top2()
                link(dve.tensor_tensor(tif[:], top[:, :, 0:2], top[:, :, 0:1].broadcast_to((P, NT, 2)), ALU.subtract))
                dve.sem_inc(exin_ok, 1)
                dve.wait_ge(ex_ok, 2)
                link(dve.tensor_reduce(zs[:], top[:, :, 2:4], AX.X, ALU.add))
                link(dve.reciprocal(rz[:], zs[:]))
                link(dve.tensor_tensor(tif[:], top[:, :, 2:4], rz[:, :, None].broadcast_to((P, NT, 2)), ALU.mult))
                for k in range(2):
                    last = dve.tensor_tensor((sel if k == 0 else dlt)[:], oh[:, :, k, :], bc(tif[:, :, k:k + 1]), ALU.mult)
                link(last)
                link(dve.tensor_tensor(gate[:], sel[:], dlt[:], ALU.add))
                dve.sem_inc(g1_ok, 1)

            def attention(plan):
                for item in plan:
                    k = item[0]
                    if k == "max":
                        row_max(*item[1:])
                    if k == "lo":
                        low(*item[1:])
                    if k == "qk" and item[1] == 1:
                        rotary(item[2])
                    if k == "vev":
                        values(*item[1:])
                    if k == "mrow":
                        max_low(*item[1:])
                    if k == "norm":
                        normalise(*item[1:])
                    if k == "res":
                        residual(*item[1:])
                    if k == "disp":
                        dispatch(item[2])
                    if k == "rcon":
                        router_constants()
                    if k == "route":
                        route()
                    if k == "keys":
                        keys()
                    if k == "pre":
                        pre(item[2])

            attention(plan0)
            dve.wait_ge(bcol_ok, 7)
            dve.sem_inc(y_ok, 2)
            with dve.Fori(0, E0 - 1, 2) as e0:
                for i in range(2):
                    dve.wait_ge(y_full, e0 + (i + 1))
                    dve.tensor_scalar(xd[:, :, bass.ds(e0 + i, 1), :].rearrange("c b e n -> c b (e n)"),
                                      bank[f"P{i}"][:, 0:NSLOT].rearrange("c (b n) -> c b n", b=NB),
                                      b2T[:, bass.ds(e0 + i, 1)], None, ALU.add).then_inc(y_ok, 1)
            attention(plan1)
            route1()
            for g in range(4):
                dve.wait_ge(b2_full, g + 1)
                last = dve.tensor_tensor(X[:, 4 * g:4 * g + 4, :], bank[f"P{g % 2}"][:].rearrange("q (t c) -> q t c", t=4),
                                         X[:, 4 * g:4 * g + 4, :], ALU.add)
                last.then_inc(b2_ok, 1)
            dve.wait_ge(b2_ok, 4)
            dve.sem_inc(gy_free, 2)
            with dve.Fori(0, E1 - 1, 2) as e0:
                for i in range(2):
                    for h in range(2):
                        dve.wait_ge(wt_full, 2 * (e0 + i) + (h + 1))
                        dve.tensor_copy(D_W[i][:, 512 * h:512 * (h + 1)], bank[f"M{h}"][:]).then_inc(wt_ok, 1)
                    for tc in range(4):
                        dve.wait_ge(gy_full, 4 * (e0 + i) + (tc + 1))
                        for tt in range(4):
                            x = X[:, 4 * tc + tt, :]
                            last = dve.scalar_tensor_tensor(out=x, in0=bank[f"P{tc % 2}"][:, P * tt:P * (tt + 1)],
                                                            scalar=gate[:, 4 * tc + tt, bass.ds(e0 + i, 1)], in1=x,
                                                            op0=ALU.mult, op1=ALU.add)
                        last.then_inc(gy_free, 1)

        @block.tensor
        def _(pe):
            mm = pe.matmul
            M0, M1 = bank["M0"], bank["M1"]
            one = ones[0:1, 0:1]
            pe.wait_ge(k_in, 16)
            for i in range(4):
                n = f"{'NNSS'[i]}{i % 2}"
                pe.wait_ge(xn_ok, 4 * (i + 1))
                for j in range(4):
                    last = pe.transpose(bank[n][:, P * j:P * (j + 1)], XN[:, 4 * i + j, :], ident)
                last.then_inc(full[n], 1)
            pe.wait_ge(w_in, 64)
            for i in range(NT):
                if i % 4 == 0:
                    pe.wait_ge(xt0_ok, i // 4 + 1)
                last = mm(bank["P0"][:, E0 * i:E0 * (i + 1)], XT[:, P * i:P * (i + 1)], Wr[:], start=True, stop=True)
            last.then_inc(full["P0"], 1)
            pe.wait_ge(brow_ok, 64)
            for i in range(2):
                last = mm(M0[:, i:i + 1], brow[0:1, i, :], one, start=True, stop=True)
            last.then_inc(full["M0"], 1)

            def bias1():
                await_free(pe, "M0", ("bias1",))
                pe.wait_ge(f_in, 16 * 17)
                pe.wait_ge(ab_ok, 1)
                mm(M0[:, 2:6], K[0:1, CO_MASK:CO_MASK + P], K[0:1, CO_TRI:CO_TRI + 1].broadcast_to((1, 4)),
                   start=True, stop=True)
                for i, n in enumerate((P, P, NKV * HD, NKV * HD)):
                    mm(M0[0:n, 2 + i:3 + i], browP[0:1, i, 0:n], one, start=True, stop=True)
                pe.transpose(M0[:, 32:64], b1raw[:], ident[0:32, 0:32])
                pe.transpose(M0[:, 64:96], u1raw[:], ident[0:32, 0:32])
                pe.transpose(M0[:, 96:104], b2raw[:], ident[0:E0, 0:E0])
                pe.transpose(M0[:, 104:112], rwr[:], ident[0:E1, 0:E1]).then_inc(full["M0"], 1)

            def cum():
                await_free(pe, "P1", ("cum",))
                pe.wait_ge(const_ok, 1)
                pe.wait_ge(sel_ok, 1)
                o = bank["P1"][:, 0:NT * E0]
                mm(o, trib[:], selb[:].rearrange("p a e -> p (a e)"), start=True, stop=False)
                mm(o.rearrange("p (b q e) -> p b q e", q=2, e=E0)[:, :, 1, :], oneb[:],
                   selb[:].rearrange("p (b q) e -> p b q e", q=2)[:, :, 0, :], start=False, stop=True)\
                    .then_inc(full["P1"], 1)

            def qk(L, b):
                x = XT[:, T * b:T * (b + 1)]
                if L == 0:
                    await_free(pe, "M1", ("qk", L, b))
                    for j in range(2):
                        last = mm(M1[:, T * j:T * (j + 1)], Wqkv[0][:, j, :], x, start=True, stop=True)
                    last.then_inc(full["M1"], 1)
                else:
                    await_free(pe, "M1", ("qk", L, b))
                    await_free(pe, "M0", ("qk", L, b))
                    for j in range(2):
                        last = mm(M1[:, T * j:T * (j + 1)], WqAB[:, j, :], x, start=True, stop=True)
                    last.then_inc(full["M1"], 1)
                    for j in range(2):
                        last = mm(M0[0:32, T * j:T * (j + 1)], WkAB[:, j, :], x, start=True, stop=True)
                    last.then_inc(full["M0"], 1)

            def val(L, b):
                n = C if L == 0 else NKV * HD
                await_free(pe, "M0", ("val", L, b))
                for q in range(TPB):
                    last = mm(M0[:, n * q:n * (q + 1)], XT[:, T * b + P * q:T * b + P * (q + 1)], Wqkv[L][:, 2, 0:n],
                              start=True, stop=True)
                last.then_inc(full["M0"], 1)

            def k_part(L, h):
                return 8 + (h // 2 if L == 0 else h // (NH // NKV))

            def nat(L, b, u):
                h, v = u // 6, u % 6
                qt, p, heads = nat_heads(h, v)
                many = len(heads)
                s = bank[f"N{u % 2}"]
                await_free(pe, f"N{u % 2}", ("nat", L, b, u))
                if u == 0:
                    pe.wait_ge(stk_in[b % NSTK], stack_in_count(L, b))
                w_ = 512 // many
                diag = s[:].rearrange("q (h k) -> q h k", h=many)[:, :, w_ - P:w_]
                mm(diag, identb[:], maskb[:, None, :].broadcast_to((P, many, P)), start=True, stop=False,
                   skip_group_check=True)
                stk = STK[b % NSTK]
                for i, head in enumerate(heads):
                    j = head // 2
                    last = mm(s[:, w_ * i:w_ * (i + 1)], stk[64 * p:64 * p + 32, j, P * qt:P * (qt + 1)],
                              stk[64 * p:64 * p + 32, k_part(L, head), 0:w_], start=False, stop=True,
                              skip_group_check=True)
                last.then_inc(full[f"N{u % 2}"], 1)

            def stack_in_count(L, b):
                s = b % NSTK
                n0 = len([x for x in range(NB) if x % NSTK == s])
                k = b // NSTK + 1
                return 32 * k if L == 0 else 32 * n0 + 64 * k

            def m_in_count(L, b):
                s = b % NSTK
                n0 = len([x for x in range(NB) if x % NSTK == s])
                return 32 * (b // NSTK + 1 + (n0 if L else 0))

            def st(L, b, g, r):
                u = 3 * g + r
                s = bank[f"S{u % 2}"]
                await_free(pe, f"S{u % 2}", ("st", L, b, g, r))
                if r == 0 and g % 2 == 0:
                    pe.wait_ge(m_in[b % NSTK][g // 2], m_in_count(L, b))
                heads = group_heads(g)[2 * r:2 * r + 2] if r < 2 else group_heads(g)
                n = 512 // len(heads)
                stk = STK[b % NSTK]
                for i, head in enumerate(heads):
                    j, p = head // 2, head % 2
                    kt = 0 if r < 2 else 1
                    last = mm(s[:, n * i:n * (i + 1)], stk[64 * p:64 * p + 34, k_part(L, head), P * kt:P * (kt + 1)],
                              stk[64 * p:64 * p + 34, j, T - n:T], start=True, stop=True)
                last.then_inc(full[f"S{u % 2}"], 1)

            def pv(L, b, g):
                n = seq(L, b)
                bk = f"P{g // 2}"
                if g % 2 == 0:
                    await_free(pe, bk, ("o", L, b, g // 2))
                if g == 0:
                    pe.wait_ge(val_ok, n + 1)
                pe.wait_ge(mask_ok, 4 * n + g + 1)
                va = VA[b % NV]
                for kt in range(2):
                    for c in range(4):
                        head = group_heads(g)[c] // (1 if L == 0 else NH // NKV)
                        o = bank[bk][32 * c:32 * c + 32, T * (g % 2) + P * kt:T * (g % 2 + 1)]
                        pr = PT[:, g, c // 2, T * (c % 2):T * (c % 2 + 1)] if kt == 0 else PT[:, g, 2, P * c:P * (c + 1)]
                        last = mm(o, va[:, kt, head, :], pr, start=(kt == 0), stop=(kt == 1))
                last.then_inc(pv_ok, 1)

            def mxt(L, b, h):
                n = seq(L, b)
                await_free(pe, "M1", ("mxt", L, b, h))
                pe.wait_ge(nm_ok, 12 * n + 6 * (h + 1))
                for q in range(TPB):
                    last = pe.transpose(M1[0:8, P * q:P * (q + 1)], NM[b % 2][:, h, q, :], ident)
                last.then_inc(full["M1"], 1)

            def otr(L, b):
                n = seq(L, b)
                pe.wait_ge(ocp_ok, 2 * n + 2)
                for q in range(TPB):
                    await_free(pe, f"P{q}", ("otr", L, b, q))
                    for g in range(4):
                        last = pe.transpose(bank[f"P{q}"][:, P * g:P * (g + 1)],
                                            OT[b % 2][:, T * g + P * q:T * g + P * (q + 1)], ident)
                    last.then_inc(full[f"P{q}"], 1)

            def ott(L, b):
                n = seq(L, b)
                await_free(pe, "P0", ("ott", L, b))
                pe.wait_ge(on_ok, 2 * n + 2)
                for q in range(TPB):
                    last = pe.transpose(bank["P0"][:, P * q:P * (q + 1)], ON[:, q, :], ident)
                last.then_inc(full["P0"], 1)

            def proj(L, b):
                n = seq(L, b)
                await_free(pe, "P1", ("proj", L, b))
                pe.wait_ge(ont_ok, n + 1)
                if n == 0:
                    pe.wait_ge(wo_in, 16 * 6)
                for q in range(TPB):
                    last = mm(bank["P1"][:, P * q:P * (q + 1)], ONT[:, P * q:P * (q + 1)], Wo[L][:], start=True, stop=True)
                last.then_inc(full["P1"], 1)

            def dsm(b):
                await_free(pe, "M0", ("dsm", 0, b))
                pe.wait_ge(dm_ok, b + 1)
                for q in range(TPB):
                    last = mm(M0[:, 0:NSLOT], XN[:, 2 * b + q, :], DM[:, q, :, :].rearrange("p e n -> p (e n)"),
                              start=(q == 0), stop=(q == 1))
                last.then_inc(full["M0"], 1)

            def gt(b, k):
                bk = "M1" if k == 0 else "M0"
                await_free(pe, bk, ("gt", 0, b, k))
                pe.wait_ge(gm_ok, b + 1)
                for j, (e, ne) in enumerate(GCH[:2] if k == 0 else GCH[2:]):
                    at, n = e * CAP, ne * CAP
                    for q in range(TPB):
                        last = pe.transpose(bank[bk][0:n, T * j + P * q:T * j + P * (q + 1)],
                                            GM[:, q, :, :].rearrange("p e n -> p (e n)")[:, at:at + n], ident)
                last.then_inc(full[bk], 1)

            def rcon():
                await_free(pe, "M0", ("rcon",))
                pe.wait_ge(rcin_ok, 2)
                mm(M0[:, 0:E1], ones, rwS[:], start=True, stop=True)
                mm(M0[:, E1:2 * E1], ones, rwB[:], start=True, stop=True).then_inc(full["M0"], 1)

            def pre(b):
                await_free(pe, "M0", ("pre", 1, b, "y"))
                for j, (e, ne) in enumerate(GCH):
                    last = pe.transpose(M0[0:ne * CAP, P * j:P * (j + 1)], xd[:, b, e:e + ne, :].rearrange("c e n -> c (e n)"),
                                        ident)
                last.then_inc(full["M0"], 1)
                await_free(pe, "M0", ("pre", 1, b, "o"))
                pe.wait_ge(ys_ok, b + 1)
                for q in range(TPB):
                    for j, n in enumerate(ne * CAP for _, ne in GCH):
                        last = mm(M0[:, P * q:P * (q + 1)], GT[0:n, b, j, P * q:P * (q + 1)], ys[0:n, j, :],
                                  start=(j == 0), stop=(j == 2))
                last.then_inc(full["M0"], 1)
                await_free(pe, "M0", ("pre", 1, b, "xt"))
                pe.wait_ge(xnb_ok, 2 * b + 2)
                for q in range(TPB):
                    last = pe.transpose(M0[:, P * q:P * (q + 1)], XN[:, 2 * b + q, :], ident)
                last.then_inc(full["M0"], 1)
                await_free(pe, "M0", ("pre", 1, b, "lg"))
                pe.wait_ge(xt_ok, b + 1)
                for q in range(TPB):
                    last = mm(M0[:, E1 * q:E1 * (q + 1)], XT[:, T * b + P * q:T * b + P * (q + 1)], rwS[:],
                              start=True, stop=True)
                last.then_inc(full["M0"], 1)

            work = {"qk": qk, "val": val, "nat": nat, "st": st, "pv": pv, "mxt": mxt, "otr": otr, "ott": ott,
                    "proj": proj}

            def attention(plan):
                for item in plan:
                    k = item[0]
                    if k in work:
                        work[k](*item[1:])
                    if k == "dsm":
                        dsm(item[2])
                    if k == "gt":
                        gt(*item[2:])
                    if k == "rcon":
                        rcon()
                    if k == "pre":
                        pre(item[2])
                    if k == "bias1":
                        bias1()
                    if k == "cum":
                        cum()

            attention(plan0)

            for n in names:
                pe.wait_ge(*released(last0[n]))
            pe.wait_ge(xd_ok, NB)
            with pe.Fori(0, E0 - 1, 2) as e0:
                for i in range(2):
                    pe.wait_ge(fw_in[i], 16 * e0 + 32)
                    x = xd[:, :, bass.ds(e0 + i, 1), :].rearrange("c b e n -> c b (e n)")
                    for m in range(HC):
                        last = mm(bank[f"{'NS'[m // 2]}{m % 2}"][:, 0:NSLOT], F_W[i][:, P * m:P * (m + 1)], x,
                                  start=True, stop=True)
                        last.then_inc(up_full, 1)
                    pe.wait_ge(y_ok, e0 + (i + 1))
                    for m in range(HC):
                        pe.wait_ge(h_ok, HC * (e0 + i) + (m + 1))
                        last = mm(bank[f"P{i}"][:, 0:NSLOT], F_W[i][:, H0 + P * m:H0 + P * (m + 1)],
                                  F_H[i][:, NSLOT * m:NSLOT * (m + 1)], start=(m == 0), stop=(m == HC - 1))
                    last.then_inc(y_full, 1)
            pe.wait_ge(y_ok, E0 + 2)
            attention(plan1)

            for n in names:
                pe.wait_ge(*released(last_use[n]))
            pe.wait_ge(g1_ok, 1)
            for g in range(4):
                if g >= 2:
                    pe.wait_ge(gT_ok, g - 1)
                for j in range(4):
                    last = pe.transpose(bank[f"N{g % 2}"][0:E1, P * j:P * (j + 1)], gate[:, 4 * g + j, :], ident)
                last.then_inc(gT_full, 1)
            for g in range(4):
                pe.wait_ge(gT_ok, g + 1)
                if g >= 2:
                    pe.wait_ge(b2_ok, g - 1)
                for j in range(4):
                    i = 4 * g + j
                    last = mm(bank[f"P{g % 2}"][:, P * j:P * (j + 1)], gT[:, P * i:P * (i + 1)], d2row[:],
                              start=True, stop=True)
                last.then_inc(b2_full, 1)
            pe.wait_ge(b2_ok, 4)
            with pe.Fori(0, E1 - 1, 2) as e0:
                for i in range(2):
                    pe.wait_ge(dw_in[i], 16 * e0 + 32)
                    for h in range(2):
                        for m in range(HC):
                            src = D_RAW[i][:, 512 * h + P * m:512 * h + P * (m + 1)]
                            last = pe.transpose(bank[f"M{h}"][:, P * m:P * (m + 1)], src, ident)
                        last.then_inc(wt_full, 1)
                    for tc in range(4):
                        if tc == 0:
                            pe.wait_ge(wt_ok, 2 * (e0 + i) + 2)
                        for m in range(HC):
                            pe.wait_ge(gu_ok, 16 * (e0 + i) + (4 * tc + m + 1))
                            mm(bank[f"{'NS'[m // 2]}{m % 2}"][:], D_W[i][:, P * m:P * (m + 1)],
                               XT[:, 512 * tc:512 * (tc + 1)], start=True, stop=True).then_inc(gu_full, 1)
                        pe.wait_ge(gu_ok, 16 * (e0 + i) + (4 * tc + 8))
                        pe.wait_ge(gy_free, 4 * (e0 + i) + (tc + 1))
                        for tt in range(4):
                            for m in range(HC):
                                last = mm(bank[f"P{tc % 2}"][:, P * tt:P * (tt + 1)],
                                          D_H[tc % 2][:, 512 * m + P * tt:512 * m + P * (tt + 1)],
                                          D_W[i][:, 512 + P * m:512 + P * (m + 1)], start=(m == 0), stop=(m == HC - 1))
                        last.then_inc(gy_full, 1)


def kernel(**inputs):
    import concourse.bacc as bacc
    from concourse.bass_utils import run_bass_kernel_spmd

    nc = bacc.Bacc("TRN2", target_bir_lowering=False, num_devices=1)
    arrays, aps = {}, {}
    for name in INPUTS:
        a = np.ascontiguousarray(inputs[name])
        arrays[f"in_{name}"] = a
        aps[name] = nc.dram_tensor(f"in_{name}", a.shape, mybir.dt.from_np(a.dtype), kind="ExternalInput").ap()
    arrays["in_table"] = constants()
    table = nc.dram_tensor("in_table", (P, NCONST), F32, kind="ExternalInput").ap()
    out = nc.dram_tensor("out_0", (NB, T, C), F32, kind="ExternalOutput").ap()
    build(nc, aps, table, out)
    r = run_bass_kernel_spmd(nc, [arrays], core_ids=[0])
    return r.results[0]["out_0"]
```

```python
from contextlib import ExitStack

import numpy as np

import concourse.bass as bass
from concourse import mybir

F32 = mybir.dt.float32
F32R = mybir.dt.float32r
BF16 = mybir.dt.bfloat16
U32 = mybir.dt.uint32
ALU = mybir.AluOpType
ACT = mybir.ActivationFunctionType
AX = mybir.AxisListType

P = 128
NB, T, C = 8, 256, 128
NT = NB * T // P
TPB = T // P
NH, HD = 16, 8
NKV = 4
E0, H0 = 8, 512
CAP = int(T / E0 * 1.25)
NSLOT = E0 * CAP
GCH = [(0, 3), (3, 3), (6, 2)]
E1, H1 = 8, 512
HC = H0 // P
EPS = 1e-5
SCALE = float(HD) ** -0.5
NEG = -1e30
NSTK = 3
NV = 3
WARM = [(0, 2, 4, 6, 8, 9, 10, 11), (0, 4, 8)]

CO_ID, CO_MASK, CO_TRI, CO_ONE = 0, P, 2 * P, 3 * P
CO_C, CO_S = 4 * P, 4 * P + T
CO_I8 = 4 * P + 2 * T
CO_IN = CO_I8 + E0
NCONST = CO_IN + CAP


def constants():
    t = np.zeros((P, NCONST), np.float32)
    r, c = np.arange(P)[:, None], np.arange(P)[None, :]
    t[:, CO_ID:CO_ID + P] = r == c
    t[:, CO_MASK:CO_MASK + P] = np.where(c > r, NEG, 0.0)
    t[:, CO_TRI:CO_TRI + P] = r < c
    t[:, CO_ONE:CO_ONE + P] = 1.0
    inv = (np.float32(1.0) / np.float32(10000.0) ** (np.arange(0, HD, 2, dtype=np.float32) / np.float32(HD))).astype(np.float32)
    ang = (np.arange(T, dtype=np.float32)[None, :] * inv[:, None]).astype(np.float32)
    cos, sin = np.cos(ang).astype(np.float32), np.sin(ang).astype(np.float32)
    for row in range(P):
        i = row % HD
        a, b = (cos, sin) if i < HD // 2 else (sin, cos)
        t[row, CO_C:CO_C + T] = a[i % (HD // 2)]
        t[row, CO_S:CO_S + T] = b[i % (HD // 2)]
    t[:, CO_I8:CO_I8 + E0] = np.arange(E0)
    t[:, CO_IN:CO_IN + CAP] = np.arange(1, CAP + 1)
    return t


def attention_plan(L):
    plan = []
    for t in range(NB + 3):
        a, b, c, d = (x if 0 <= x < NB else None for x in (t, t - 1, t - 2, t - 3))

        def add(kind, batch, *rest):
            if batch is not None:
                plan.append((kind, L, batch, *rest))

        if L == 1 and t == 0:
            plan += [(k, L, b) for k in ("py", "po", "px", "pl") for b in range(2)]
        e = t + 1 if L == 1 and 0 < t < NB - 1 else None
        for u in range(12):
            if u == 0:
                add("qk", a)
                add("hi", a)
            if u == (0 if L == 0 else 1):
                add("lo", a)
            add("nat", b, u)
            add("st", c, u // 3, u % 3)
            add("max", b, u)
            add("exp", c, u // 3, u % 3)
            if u % 3 == 2:
                add("msk", c, u // 3)
            if u == 0:
                add("pv", d, 3)
            if u == 1:
                add("mxt", c, 1)
                add("mrow", c, 1)
                add("stack", a)
                add("ocp", d, 1)
            if u == 2:
                add("val", a)
            if u == 3:
                add("vev", a)
                add("otr", d)
                add("norm", d)
                if L == 0 and t == 0:
                    plan += [("lg",), ("route",)]
                if L == 0 and t == 1:
                    plan += [("cum",), ("keys",)]
            if u == 4:
                add("py", e)
                if L == 0:
                    add("disp", b)
            if u == 5 and L == 0 and t == 3:
                plan.append(("bias1",))
            if u == 5:
                add("ott", d)
                add("po", e)
            if u == 6:
                add("oev", d)
                add("mxt", b, 0)
                add("mrow", b, 0)
                if L == 0:
                    add("dsm", b)
                    add("dse", b)
            if u == 7:
                add("proj", d)
            if u == 8:
                add("res", d)
                add("pv", c, 0)
                if L == 0:
                    add("gt", b, 0)
                    add("gte", b, 0)
            if u == 9:
                add("pv", c, 1)
                add("px", e)
                if L == 0:
                    add("gt", b, 1)
                    add("gte", b, 1)
            if u == 10:
                add("ocp", c, 0)
                add("pl", e)
            if u == 11:
                add("pv", c, 2)
        if L == 1 and t == NB:
            plan.append(("route1",))
    return plan


def group_heads(g):
    return [8 * (g // 2) + g % 2 + 2 * c for c in range(4)]


def nat_heads(h, v):
    if v < 2:
        return 0, v, group_heads(2 * h + v)
    return 1, v % 2, group_heads(2 * h + v % 2)[2 * (v // 2 - 1):2 * (v // 2)]


def bank_uses(item):
    kind = item[0]
    if kind == "xt":
        return [("N0 N1 S0 S1".split()[item[1] % 4], item)]
    if kind == "lg":
        return [("P0", item)]
    if kind == "cum":
        return [("P1", item)]
    if kind in ("bias", "bias1", "rcon"):
        return [("M0", item)]
    if kind == "nat":
        return [(f"N{item[3] % 2}", item)]
    if kind == "st":
        return [(f"S{(3 * item[3] + item[4]) % 2}", item)]
    if kind == "pv":
        return [(f"P{item[3] // 2}", ("o", item[1], item[2], item[3] // 2))]
    if kind == "otr":
        return [("P0", item + (0,)), ("P1", item + (1,))]
    if kind == "ott":
        return [("P0", item)]
    if kind == "proj":
        return [("P1", item)]
    if kind == "qk":
        return [("M1", item)] if item[1] == 0 else [("M1", item), ("M0", item)]
    if kind == "val":
        return [("M0", item)]
    if kind == "mxt":
        return [("M1", item)]
    if kind == "dsm":
        return [("M0", item)]
    if kind == "gt":
        return [("M1" if item[3] == 0 else "M0", item)]
    if kind in ("py", "po", "px", "pl"):
        return [(f"M{item[2] % 2}", item)]
    return []


INPUTS = [
    "L0_attn_x", "L0_attn_Wq", "L0_attn_bq", "L0_attn_Wk", "L0_attn_bk", "L0_attn_Wv", "L0_attn_bv",
    "L0_attn_Wo", "L0_attn_bo", "L0_ffn_Wr", "L0_ffn_W1", "L0_ffn_b1", "L0_ffn_W2", "L0_ffn_b2",
    "L1_attn_Wq", "L1_attn_bq", "L1_attn_Wk", "L1_attn_bk", "L1_attn_Wv", "L1_attn_bv", "L1_attn_Wo",
    "L1_attn_bo", "L1_ffn_ln_scale", "L1_ffn_ln_bias", "L1_ffn_router_w", "L1_ffn_router_b",
    "L1_ffn_up_w", "L1_ffn_up_b", "L1_ffn_down_w", "L1_ffn_down_b"]


def build(nc, w, table, out):
    ctx = ExitStack()
    with ctx:
        def sb(name, shape, dt=F32):
            return ctx.enter_context(nc.sbuf_tensor(name, shape, dt))

        def sem(name):
            return ctx.enter_context(nc.semaphore(name))

        def dram(name, shape):
            return nc.dram_tensor(name, shape, F32, kind="Internal").ap()

        X = sb("X", [P, NT, C])
        XN = sb("XN", [P, NT, C])
        XT = sb("XT", [P, NT * P])
        K = sb("consts", [P, NCONST])
        ident, ones = K[:, CO_ID:CO_ID + P], K[:, CO_ONE:CO_ONE + P]
        cosr, sinr = K[:, CO_C:CO_C + T], K[:, CO_S:CO_S + T]
        identb, maskb, trib, oneb = (sb(n, [P, P], BF16) for n in ("identb", "maskb", "trib", "oneb"))
        Wqkv = [sb(f"Wqkv{L}", [P, 3, C]) for L in range(2)]
        Wo = [sb(f"Wo{L}", [P, C]) for L in range(2)]
        Wr = sb("Wr", [P, E0])
        WqAB = sb("WqAB", [P, 2, C])
        WkAB = sb("WkAB", [P, 2, NKV * HD])
        brow = sb("brow", [1, 4, C])
        browP = sb("browP", [1, 4, C])
        bcol = sb("bcol", [P, 6])
        bvb = [sb(f"bvb{L}", [P, C]) for L in range(2)]
        bob = [sb(f"bob{L}", [P, C]) for L in range(2)]
        b1raw = sb("b1raw", [E0 * HC, P])
        b2raw = sb("b2raw", [E0, C])
        b1T = sb("b1T", [P, E0 * HC])
        b2T = sb("b2T", [P, E0])
        u1raw = sb("u1raw", [E1 * HC, P])
        u1T = sb("u1T", [P, E1 * HC])
        ucol = [sb(f"ucol{i}", [P, HC]) for i in range(2)]
        d2row = sb("d2row", [E1, C])
        lns, lnb = sb("lns", [P, 1]), sb("lnb", [P, 1])
        rwr = sb("rwr", [E1, C])
        rwS, rwB = sb("rwS", [P, E1]), sb("rwB", [P, E1])
        rbb = sb("rbb", [P, E1])
        rc = sb("rc", [P, 2, E1])

        stats = sb("stats", [P, NT, 6])
        mv = sb("mv", [P, NT, 2])
        vpe = sb("vpe", [P, NT])
        rstd = sb("rstd", [P, NT])
        mhalf = sb("mhalf", [P, NT])
        stats2, mv2 = sb("stats2", [P, NT, 6]), sb("mv2", [P, NT, 2])
        rstd2 = sb("rstd2", [P, NT])

        XQ = [sb(f"XQ{i}", [P, 4, T], F32R) for i in range(2)]
        ROT = [sb(f"ROT{i}", [P, 4, T]) for i in range(2)]
        STK = [sb(f"STK{i}", [P, 16, T], F32R) for i in range(NSTK)]
        NM = [sb(f"NM{i}", [P, 2, TPB, NH // 2]) for i in range(2)]
        MS = [sb(f"MS{i}", [NH // 2, 2, T], F32R) for i in range(2)]
        PT = sb("PT", [P, 4, 3, 512])
        VA = [sb(f"VA{i}", [P, TPB, NH, 32]) for i in range(NV)]
        OT = [sb(f"OT{i}", [P, 4 * T]) for i in range(2)]
        rcp = sb("rcp", [P, TPB, NH])
        ON = sb("ON", [P, TPB, C])
        ONT = sb("ONT", [P, T])

        lg = sb("lg", [P, NT, E0])
        top = sb("top", [P, NT, 8])
        tix = sb("tix", [P, NT, 8], U32)
        tif = sb("tif", [P, NT, 2])
        oh = sb("oh", [P, NT, 2, E0])
        sel = sb("sel", [P, NT, E0])
        selb = sb("selb", [P, NT, E0], BF16)
        dlt, ex = sb("dlt", [P, NT, E0]), sb("ex", [P, NT, E0])
        zs, rz = sb("zs", [P, NT]), sb("rz", [P, NT])
        gate = sb("gate", [P, NT, E0])
        key = sb("key", [P, NT, E0])
        DM = sb("DM", [P, TPB, E0, CAP])
        GM = sb("GM", [P, TPB, E0, CAP])
        GT = sb("GT", [P, NB, 3, T])
        xd = sb("xd", [P, NB, E0, CAP])
        ys = sb("ys", [P, 3, P])

        PTf = PT[:, :, :, :].rearrange("p a b c -> p (a b c)")
        F_W = [ROT[i][:, :, :].rearrange("p a t -> p (a t)") for i in range(2)]
        F_H = [PTf[:, 2048 + 1280 * i:2048 + 1280 * (i + 1)] for i in range(2)]
        GTf = GT[:, :, :, :].rearrange("p a b c -> p (a b c)")
        XDf = xd[:, :, :, :].rearrange("p a b c -> p (a b c)")
        gT = XDf[0:E1, 0:NT * P]
        D_RAW = [PTf[:, 1024 * i:1024 * (i + 1)] for i in range(2)]
        D_W = [PTf[:, 2048 + 512 * i:2048 + 512 * (i + 1)] for i in range(2)]
        STKf = [x[:, :, :].rearrange("p a t -> p (a t)") for x in STK]
        XH, XL = STKf[0][:, 0:NT * P], STKf[1][:, 0:NT * P]
        WH = [STKf[2][:, H1 * i:H1 * (i + 1)] for i in range(2)]
        WL = [STKf[2][:, H1 * (2 + i):H1 * (3 + i)] for i in range(2)]
        D_H = [GTf[:, 2048 * i:2048 * (i + 1)] for i in range(2)]

        names = "N0 N1 S0 S1 P0 P1 M0 M1".split()
        bank = {n: ctx.enter_context(nc.psum_tensor(f"ps_{n}", [P, 512], F32)) for n in names}

        scr = [[dram(f"scr{L}_{b}", (2, P, 4, T)) for b in range(NB)] for L in range(2)]
        scm = [[[dram(f"scm{L}_{b}_{h}", (NH // 2, 2, T)) for h in range(2)] for b in range(NB)] for L in range(2)]

        full = {n: sem(f"full_{n}") for n in names}
        x0_in, x_in, k_in, w_in, wo_in, f_in = (sem(n) for n in ("x0_in", "x_in", "k_in", "w_in", "wo_in", "f_in"))
        const_ok = sem("const_ok")
        va_ok, stk_ok = sem("va_ok"), sem("stk_ok")
        brow_ok = sem("brow_ok")
        bcol_ok = sem("bcol_ok")
        mv_ok, rstd_ok, xn_ok, xt_ok = sem("mv_ok"), sem("rstd_ok"), sem("xn_ok"), sem("xt_ok")
        xbo_ok = sem("xbo_ok")
        dstep = sem("dstep")
        pstep = sem("pstep")
        vpea_ok, vpeb_ok = sem("vpea_ok"), sem("vpeb_ok")
        sel_ok, exin_ok, ex_ok, key_ok, gate_ok, lg_ok, xt0_ok = (
            sem(n) for n in ("sel_ok", "exin_ok", "ex_ok", "key_ok", "gate_ok", "lg_ok", "xt0_ok"))
        qhi_ok, qlo_ok, rot_ok, rsub_ok = sem("qhi_ok"), sem("qlo_ok"), sem("rot_ok"), sem("rsub_ok")
        scr_w = [sem(f"scr_w{i}") for i in range(2)]
        stk_in = [sem(f"stk_in{i}") for i in range(NSTK)]
        val_ok = sem("val_ok")
        nm_ok, mhi_ok, mlo_ok = sem("nm_ok"), sem("mhi_ok"), sem("mlo_ok")
        scm_w = [sem(f"scm_w{i}") for i in range(2)]
        m_in = [[sem(f"m_in{i}{h}") for h in range(2)] for i in range(NSTK)]
        exp_ok, mask_ok, pv_ok = sem("exp_ok"), sem("mask_ok"), sem("pv_ok")
        ocp_ok, on_ok, ont_ok = sem("ocp_ok"), sem("on_ok"), sem("ont_ok")
        dm_ok, gm_ok, gt_ok, xd_ok = (sem(n) for n in ("dm_ok", "gm_ok", "gt_ok", "xd_ok"))
        ab_ok = sem("ab_ok")
        x1_ok = sem("x1_ok")
        fw_in = [sem(f"fw_in{i}") for i in range(2)]
        up_full, up_free, h_ok, y_full, y_ok = (sem(n) for n in ("up_full", "up_free", "h_ok", "y_full", "y_ok"))
        ys_ok, x2_ok, mvb_ok, rstdb_ok, xnb_ok, ybo_ok = (sem(n) for n in ("ys_ok", "x2_ok", "mvb_ok", "rstdb_ok", "xnb_ok", "ybo_ok"))
        lg1_ok = sem("lg1_ok")
        mvc_ok, rstdc_ok, rc_ok, rcin_ok = sem("mvc_ok"), sem("rstdc_ok"), sem("rc_ok"), sem("rcin_ok")
        g1_ok = sem("g1_ok")
        dw_in = [sem(f"dw_in{i}") for i in range(2)]
        wt_full, wt_ok, gu_full, gu_ok, gy_full, gy_free, gT_full, gT_ok, b2_full, b2_ok = (
            sem(n) for n in ("wt_full", "wt_ok", "gu_full", "gu_ok", "gy_full", "gy_free", "gT_full", "gT_ok",
                             "b2_full", "b2_ok"))
        ucol_ok = sem("ucol_ok")
        xh_ok, xl_ok, wh_ok = sem("xh_ok"), sem("xl_ok"), sem("wh_ok")
        out_sem = sem("out_sem")

        prologue = [("bias",)] + [("xt", i) for i in range(4)]
        plan0 = attention_plan(0)
        at = plan0.index(("pv", 0, NB - 1, 3))
        plan0, tail = plan0[:at], plan0[at:]
        plan1 = attention_plan(1)
        plan1 = [("rcon",)] + plan1[:2] + tail[:2] + plan1[2:4] + tail[2:6] + plan1[4:6] + tail[6:] + plan1[6:]
        at = plan1.index(("pv", 1, NB - 1, 3))
        plan1, tail1 = plan1[:at], plan1[at:]

        def seq(L, b):
            return L * NB + b

        def released(use):
            kind = use[0]
            if kind == "xt":
                return xt0_ok, use[1] + 1
            if kind in ("lg", "cum", "bias", "bias1", "rcon"):
                return {"lg": (lg_ok, 1), "cum": (key_ok, 1), "bias": (bcol_ok, 1), "bias1": (bcol_ok, 7),
                        "rcon": (rc_ok, 1)}[kind]
            L, b, n = use[1], use[2], seq(use[1], use[2])
            if kind == "nat":
                return nm_ok, 12 * n + use[3] + 1
            if kind == "st":
                return exp_ok, 12 * n + 3 * use[3] + use[4] + 1
            if kind == "o":
                return ocp_ok, 2 * n + use[3] + 1
            if kind == "otr":
                return on_ok, 2 * n + use[3] + 1
            if kind == "qk":
                return (qlo_ok, n + 1) if L == 0 else (rot_ok, b + 1)
            if kind == "mxt":
                return mlo_ok, 2 * n + use[3] + 1
            if kind == "gt":
                return gt_ok, 2 * b + use[3] + 1
            if kind in ("py", "po", "px", "pl"):
                return {"py": ys_ok, "po": x2_ok, "px": xt_ok, "pl": lg1_ok}[kind], b + 1
            return {"ott": (ont_ok, n + 1), "proj": (x1_ok, n + 1), "val": (val_ok, n + 1), "dsm": (xd_ok, b + 1)}[kind]

        def back(L, b, k):
            n = seq(L, b) - k
            return n // NB, n % NB

        before, filled, last_use, count = {}, {}, {}, dict.fromkeys(names, 0)

        def lay(plan):
            for item in plan:
                for n, use in bank_uses(item):
                    if (n, use) in filled:
                        continue
                    before[n, use] = last_use.get(n)
                    last_use[n] = use
                    if use[0] == "o":
                        filled[n, use] = pv_ok, 4 * seq(use[1], use[2]) + 2 * use[3] + 2
                    else:
                        count[n] += 1
                        filled[n, use] = full[n], count[n]

        lay(prologue + plan0)
        last0 = dict(last_use)
        lay(plan1 + tail1)

        def await_free(eng, n, use):
            if before[n, use] is not None:
                eng.wait_ge(*released(before[n, use]))

        def await_full(eng, n, use):
            eng.wait_ge(*filled[n, use])

        x_d = w["L0_attn_x"].rearrange("b (q p) c -> p (b q) c", p=P)
        out_d = out.rearrange("b (q p) c -> p (b q) c", p=P)

        def row(name):
            return w[name].rearrange("(a c) -> a c", a=1)

        def down_rows(name, n):
            return row(name).broadcast_to((P, n))

        def load_wo(eng, L, sem):
            for g in range(4):
                src = w[f"L{L}_attn_Wo"].rearrange("(h c p d) n -> h p c d n", h=2, p=2, d=HD)[g // 2, g % 2]
                eng.dma_start(Wo[L][32 * g:32 * g + 32, :], src).then_inc(sem, 16)

        block = ctx.enter_context(nc.Block())

        @block.sync
        def _(sp):
            sp.dma_start(X[:, 0:4, :], x_d[:, 0:4, :]).then_inc(x0_in, 16)
            sp.dma_start(X[:, 4:NT, :], x_d[:, 4:NT, :]).then_inc(x_in, 16)
            sp.dma_start(K[:], table).then_inc(k_in, 16)
            sp.dma_start(Wr[:], w["L0_ffn_Wr"]).then_inc(w_in, 16)
            sp.dma_start(Wqkv[0][:, 0, :], w["L0_attn_Wq"]).then_inc(w_in, 16)
            sp.dma_start(Wqkv[0][:, 1, :], w["L0_attn_Wk"]).then_inc(w_in, 16)
            sp.dma_start(Wqkv[0][:, 2, :], w["L0_attn_Wv"]).then_inc(w_in, 16)

            def stack(L, b):
                n, i, s = seq(L, b), b % 2, b % NSTK
                rows = P if L == 0 else NKV * HD
                xq = XQ[i][:].bitcast(F32)
                sp.wait_ge(qlo_ok, n + 1)
                for part in range(2):
                    sp.dma_start(scr[L][b][0][:, 2 * part:2 * part + 2, :],
                                 xq[:, part:part + 1, :].broadcast_to((P, 2, T))).then_inc(scr_w[i], 16)
                sp.dma_start(scr[L][b][1][0:rows].rearrange("r (e s) t -> r e (s t)", e=2),
                             xq[0:rows, 2:4, :].rearrange("r s t -> r (s t)")[:, None, :]
                             .broadcast_to((rows, 2, 2 * T))).then_inc(scr_w[i], 16)
                sp.wait_ge(scr_w[i], 48 * (n // 2 + 1))
                if b >= NSTK:
                    await_full(sp, "S1", ("st", L, b - NSTK, 3, 2))
                else:
                    sp.wait_ge(stk_ok, (2 if L == 0 else 5) * NSTK)
                stk = STK[s][:].bitcast(F32)
                for p in range(2):
                    if L == 0:
                        sp.dma_start(stk[64 * p:64 * p + 32, :, :],
                                     scr[L][b].rearrange("k (j p d) s t -> p (d s) (k j) t", p=2, d=HD)[p])\
                          .then_inc(stk_in[s], 16)
                    else:
                        sp.dma_start(stk[64 * p:64 * p + 32, 0:8, :],
                                     scr[L][b][0].rearrange("(j p d) s t -> p (d s) j t", p=2, d=HD)[p])\
                          .then_inc(stk_in[s], 16)
                        sp.dma_start(stk[64 * p:64 * p + 32, 8 + NKV * p:8 + NKV * (p + 1), :],
                                     scr[L][b][1][0:rows].rearrange("(j d) s t -> (d s) j t", d=HD))\
                          .then_inc(stk_in[s], 16)

            def mrow(L, b, h):
                n = 2 * seq(L, b) + h
                sp.wait_ge(mlo_ok, n + 1)
                sp.dma_start(scm[L][b][h], MS[h][:].bitcast(F32)).then_inc(scm_w[h], 16)
                sp.wait_ge(scm_w[h], 16 * (seq(L, b) + 1))
                for p in range(2):
                    sp.dma_start(STK[b % NSTK][64 * p + 32:64 * p + 34, 4 * h:4 * h + 4, :].bitcast(F32),
                                 scm[L][b][h].rearrange("(j p) s t -> p s j t", p=2)[p])\
                      .then_inc(m_in[b % NSTK][h], 16)

            def attention(plan):
                for item in plan:
                    if item[0] == "stack":
                        stack(*item[1:])
                    if item[0] == "mrow":
                        mrow(*item[1:])

            first = plan0.index(("stack", 0, 0)) + 1
            attention(plan0[:first])
            for e in range(2):
                sp.dma_start(F_W[e][:, 0:H0], w["L0_ffn_W1"][e]).then_inc(fw_in[e], 16)
                sp.dma_start(F_W[e][:, H0:].rearrange("p (m c) -> p m c", m=HC),
                             w["L0_ffn_W2"][e].rearrange("(m p) c -> p m c", p=P)).then_inc(fw_in[e], 16)
            attention(plan0[first:])
            with sp.Fori(2, E0 - 1, 2) as e0:
                for i in range(2):
                    sp.wait_ge(y_full, e0 + (i - 1))
                    sp.dma_start(F_W[i][:, 0:H0], w["L0_ffn_W1"][bass.ds(e0 + i, 1)].rearrange("a p n -> (a p) n"))\
                      .then_inc(fw_in[i], 16)
                    sp.dma_start(F_W[i][:, H0:].rearrange("p (m c) -> p m c", m=HC),
                                 w["L0_ffn_W2"][bass.ds(e0 + i, 1)].rearrange("a (m p) c -> p (a m) c", p=P))\
                      .then_inc(fw_in[i], 16)
            attention(plan1)

            def expert_raw(e, i, many):
                up = w["L1_ffn_up_w"][bass.ds(e, 1)].rearrange("a (m p) c -> p (a m) c", p=P) if many else \
                    w["L1_ffn_up_w"][e].rearrange("(m p) c -> p m c", p=P)
                dn = w["L1_ffn_down_w"][bass.ds(e, 1)].rearrange("a p n -> (a p) n") if many else \
                    w["L1_ffn_down_w"][e]
                sp.dma_start(D_RAW[i][:, 0:H1].rearrange("p (m c) -> p m c", m=HC), up).then_inc(dw_in[i], 16)
                sp.dma_start(D_RAW[i][:, H1:], dn).then_inc(dw_in[i], 16)

            sp.wait_ge(pv_ok, 8 * NB - 1)
            for e in range(2):
                expert_raw(e, e, False)
            with sp.Fori(2, E1 - 1, 2) as e0:
                for i in range(2):
                    sp.wait_ge(wt_full, 2 * (e0 + (i - 1)))
                    expert_raw(e0 + i, i, True)
            for tc in range(4):
                sp.wait_ge(gy_free, E1 * 4 - 4 + 2 + tc + 1)
                sp.dma_start(out_d[:, 4 * tc:4 * tc + 4, :], X[:, 4 * tc:4 * tc + 4, :]).then_inc(out_sem, 16)
            sp.wait_ge(out_sem, 64)

        @block.gpsimd
        def _(pool):
            pool.memset(mhalf[:], -0.5).then_inc(pstep, 1)
            def ones_rows(i):
                for p in range(2):
                    pool.memset(STK[i][64 * p + 32:64 * p + 34, 8:16, :].bitcast(F32), 1.0).then_inc(stk_ok, 1)
                    pool.wait_ge(stk_ok, 2 * i + p + 1)

            pool.wait_ge(pstep, 1)
            ones_rows(0)
            pool.wait_ge(mv_ok, 1)
            pool.tensor_scalar(vpe[:], mv[:, :, 1], EPS, 1.0, ALU.add, ALU.mult).then_inc(pstep, 1)
            pool.wait_ge(pstep, 2)
            pool.tensor_tensor(rstd[:], vpe[:], mhalf[:], ALU.pow).then_inc(rstd_ok, 1)
            pool.wait_ge(rstd_ok, 1)
            for i in range(1, NSTK):
                ones_rows(i)
            pool.wait_ge(xn_ok, NT)
            pool.wait_ge(wo_in, 16 * 6)
            pool.tensor_tensor(X[:], X[:], bob[0][:, None, :].broadcast_to((P, NT, C)), ALU.add).then_inc(xbo_ok, 1)
            pool.dma_start(b1raw[:], w["L0_ffn_b1"].rearrange("e (m p) -> (e m) p", p=P)).then_inc(f_in, 16)
            pool.dma_start(b2raw[:], w["L0_ffn_b2"]).then_inc(f_in, 16)
            pool.dma_start(u1raw[:], w["L1_ffn_up_b"].rearrange("e (m p) -> (e m) p", p=P)).then_inc(f_in, 16)
            pool.dma_start(d2row[:], w["L1_ffn_down_b"]).then_inc(f_in, 16)
            pool.dma_start(rwr[:], w["L1_ffn_router_w"]).then_inc(f_in, 16)
            pool.dma_start(Wqkv[1][:, 0, :], w["L1_attn_Wq"]).then_inc(f_in, 16)
            pool.dma_start(Wqkv[1][:, 1, 0:NKV * HD], w["L1_attn_Wk"]).then_inc(f_in, 16)
            pool.dma_start(Wqkv[1][:, 2, 0:NKV * HD], w["L1_attn_Wv"]).then_inc(f_in, 16)
            load_wo(pool, 1, f_in)
            pool.dma_start(bvb[1][:, 0:NKV * HD], down_rows("L1_attn_bv", NKV * HD)).then_inc(f_in, 16)
            pool.dma_start(bob[1][:], down_rows("L1_attn_bo", C)).then_inc(f_in, 16)
            pool.dma_start(rbb[:], down_rows("L1_ffn_router_b", E1)).then_inc(f_in, 16)
            pool.dma_start(lns[:], w["L1_ffn_ln_scale"].rearrange("(c a) -> c a", a=1)).then_inc(f_in, 16)
            pool.dma_start(lnb[:], w["L1_ffn_ln_bias"].rearrange("(c a) -> c a", a=1)).then_inc(f_in, 16)

            def split_columns():
                pool.wait_ge(f_in, 16 * 17)
                pool.wait_ge(brow_ok, 64)
                for a in range(2):
                    pool.tensor_copy(WqAB[:, a, :].rearrange("c (h r i) -> c h r i", r=2, i=4),
                                     Wqkv[1][:, 0, :].rearrange("c (h i a) -> c h i a", i=4, a=2)[:, :, None, :, a]
                                     .broadcast_to((P, NH, 2, 4)))
                    pool.tensor_copy(WkAB[:, a, :].rearrange("c (h r i) -> c h r i", r=2, i=4),
                                     Wqkv[1][:, 1, 0:NKV * HD].rearrange("c (h i a) -> c h i a", i=4, a=2)[:, :, None, :, a]
                                     .broadcast_to((P, NKV, 2, 4)))
                    pool.tensor_copy(browP[0:1, a, :].rearrange("c (h r i) -> c h r i", r=2, i=4),
                                     brow[0:1, 2, :].rearrange("c (h i a) -> c h i a", i=4, a=2)[:, :, None, :, a]
                                     .broadcast_to((1, NH, 2, 4)))
                    last = pool.tensor_copy(browP[0:1, 2 + a, 0:NKV * HD].rearrange("c (h r i) -> c h r i", r=2, i=4),
                                            brow[0:1, 3, 0:NKV * HD].rearrange("c (h i a) -> c h i a", i=4, a=2)[:, :, None, :, a]
                                            .broadcast_to((1, NKV, 2, 4)))
                last.then_inc(ab_ok, 1)

            def mask(L, b, g):
                n = 4 * seq(L, b) + g
                pool.wait_ge(exp_ok, 3 * (n + 1))
                diag = [PT[:, g, 0:2, :].rearrange("k r (i q) -> k (r i) q", i=2)[:, :, 0:P],
                        PT[:, g, 2, :].rearrange("k (i q) -> k i q", i=4)]
                for v in diag:
                    last = pool.affine_select(out=v, in_=v, compare_op=ALU.is_ge, fill=0.0, base=0,
                                              pattern=[[0, 4], [1, P]], channel_multiplier=-1)
                last.then_inc(mask_ok, 1)

            def gated(b):
                if b > 0:
                    await_full(pool, "M0", ("gt", 0, b - 1, 1))
                pool.wait_ge(dm_ok, b + 1)
                pool.wait_ge(gate_ok, 1)
                pool.tensor_tensor(GM[:], DM[:], gate[:, 2 * b:2 * b + 2, :, None].broadcast_to((P, TPB, E0, CAP)),
                                   ALU.mult).then_inc(gm_ok, 1)

            def norm_a(b):
                s = slice(2 * b, 2 * b + 2)
                pool.wait_ge(mvb_ok, b + 1)
                pool.tensor_scalar(vpe[:, s], mv[:, s, 1], EPS, 1.0, ALU.add, ALU.mult).then_inc(vpea_ok, 1)
                pool.wait_ge(vpea_ok, b + 1)
                pool.tensor_tensor(rstd[:, s], vpe[:, s], mhalf[:, s], ALU.pow).then_inc(rstdb_ok, 1)

            def bias_out(b):
                s = slice(2 * b, 2 * b + 2)
                pool.wait_ge(xnb_ok, 2 * (b + 1))
                pool.tensor_tensor(X[:, s, :], X[:, s, :], bob[1][:, None, :].broadcast_to((P, TPB, C)), ALU.add)\
                    .then_inc(ybo_ok, 1)

            def norm_b(b):
                s = slice(2 * b, 2 * b + 2)
                pool.wait_ge(mvc_ok, b + 1)
                pool.tensor_scalar(vpe[:, s], mv2[:, s, 1], EPS, 1.0, ALU.add, ALU.mult).then_inc(vpeb_ok, 1)
                pool.wait_ge(vpeb_ok, b + 1)
                pool.tensor_tensor(rstd2[:, s], vpe[:, s], mhalf[:, s], ALU.pow).then_inc(rstdc_ok, 1)

            def rotate(b):
                n, i = b, b % 2
                pool.wait_ge(rot_ok, n + 1)
                for j, rows in ((0, P), (2, NKV * HD)):
                    last = pool.tensor_tensor(ROT[i][0:rows, j, :], ROT[i][0:rows, j, :], ROT[i][0:rows, j + 1, :],
                                              ALU.subtract)
                last.then_inc(rsub_ok, 1)

            for item in plan0:
                if item[0] == "msk":
                    mask(*item[1:])
                if item[0] == "disp":
                    gated(item[2])
                if item[0] == "cum":
                    split_columns()
            await_full(pool, "S1", ("st", 0, NB - 1, 3, 2))
            for i in range(NSTK):
                pool.memset(STK[i][:].bitcast(F32), 0.0).then_inc(stk_ok, 1)
            for i in range(NSTK):
                for p in range(2):
                    pool.wait_ge(stk_ok, 3 * NSTK + 2 * i + p)
                    pool.memset(STK[i][64 * p + 32:64 * p + 34, 8 + NKV * p:8 + NKV * (p + 1), :].bitcast(F32), 1.0)\
                        .then_inc(stk_ok, 1)
            pool.wait_ge(stk_ok, 5 * NSTK)
            for item in plan1:
                if item[0] == "msk":
                    mask(*item[1:])
                if item[0] == "po":
                    norm_a(item[2])
                if item[0] == "px":
                    bias_out(item[2])
                if item[0] == "pl":
                    norm_b(item[2])
                if item[0] == "qk":
                    rotate(item[2])

        @block.scalar
        def _(act):
            act.wait_ge(x_in, 16)
            act.wait_ge(k_in, 16)
            names_rows = ["L0_attn_bq", "L0_attn_bk", "L1_attn_bq"]
            for i, n in enumerate(names_rows):
                act.dma_start(brow[0:1, i, :], row(n)).then_inc(brow_ok, 16)
            act.dma_start(brow[0:1, 3, 0:NKV * HD], row("L1_attn_bk")).then_inc(brow_ok, 16)
            act.dma_start(bvb[0][:], down_rows("L0_attn_bv", C)).then_inc(wo_in, 16)
            load_wo(act, 0, wo_in)
            act.dma_start(bob[0][:], down_rows("L0_attn_bo", C)).then_inc(wo_in, 16)
            await_full(act, "M0", ("bias",))
            act.activation(bcol[:, 0:2], bank["M0"][:, 0:2], ACT.Copy).then_inc(bcol_ok, 1)
            for i in range(4):
                n = f"{'NNSS'[i]}{i % 2}"
                await_full(act, n, ("xt", i))
                act.activation(XT[:, 512 * i:512 * (i + 1)], bank[n][:], ACT.Copy).then_inc(xt0_ok, 1)

            def bias1():
                await_full(act, "M0", ("bias1",))
                act.activation(bcol[:, 2:6], bank["M0"][:, 2:6], ACT.Copy).then_inc(bcol_ok, 1)
                act.activation(b1T[:], bank["M0"][:, 32:64], ACT.Copy).then_inc(bcol_ok, 1)
                act.activation(u1T[:], bank["M0"][:, 64:96], ACT.Copy).then_inc(bcol_ok, 1)
                act.activation(b2T[:], bank["M0"][:, 96:104], ACT.Copy).then_inc(bcol_ok, 1)
                act.activation(rwS[:], bank["M0"][:, 104:112], ACT.Copy).then_inc(bcol_ok, 1)
                act.activation(rwB[:], bank["M0"][:, 104:112], ACT.Copy).then_inc(bcol_ok, 1)

            def route():
                act.wait_ge(exin_ok, 1)
                act.activation(ex[:], dlt[:], ACT.Exp).then_inc(ex_ok, 1)

            def route1():
                act.wait_ge(exin_ok, 2)
                act.activation(top[:, :, 2:4], tif[:], ACT.Exp).then_inc(ex_ok, 1)

            def high(L, b):
                n, i = seq(L, b), b % 2
                if n >= 2:
                    act.wait_ge(scr_w[i], 48 * (n // 2))
                if L == 0:
                    act.wait_ge(bcol_ok, 1)
                    await_full(act, "M1", ("qk", L, b))
                    act.activation(XQ[i][:, 0, :], bank["M1"][:, 0:T], ACT.Identity, bias=bcol[:, 0:1])
                    act.activation(XQ[i][:, 2, :], bank["M1"][:, T:2 * T], ACT.Identity, bias=bcol[:, 1:2])\
                        .then_inc(qhi_ok, 1)
                else:
                    act.wait_ge(rsub_ok, b + 1)
                    act.activation(XQ[i][:, 0, :], ROT[i][:, 0, :], ACT.Copy)
                    act.activation(XQ[i][0:32, 2, :], ROT[i][0:32, 2, :], ACT.Copy).then_inc(qhi_ok, 1)

            def exps(L, b, g, r):
                n, u = 4 * seq(L, b) + g, 3 * g + r
                s = f"S{u % 2}"
                if r == 0 and n >= 4:
                    act.wait_ge(pv_ok, n - 3)
                await_full(act, s, ("st", L, b, g, r))
                act.activation(PT[:, g, r, :], bank[s][:], ACT.Exp, scale=SCALE).then_inc(exp_ok, 1)

            def max_high(L, b, h):
                n = 2 * seq(L, b) + h
                if n >= 2:
                    act.wait_ge(scm_w[h], 16 * seq(L, b))
                await_full(act, "M1", ("mxt", L, b, h))
                act.activation(MS[h][:, 0, :], bank["M1"][0:NH // 2, 0:T], ACT.Copy).then_inc(mhi_ok, 1)

            def copy_o(L, b, h):
                n = seq(L, b)
                if n >= 2 and h == 0:
                    await_full(act, "P1", ("otr", *back(L, b, 2), 1))
                p = f"P{h}"
                await_full(act, p, ("o", L, b, h))
                act.activation(OT[b % 2][:, 512 * h:512 * (h + 1)], bank[p][:], ACT.Copy).then_inc(ocp_ok, 1)

            def copy_ont(L, b):
                n = seq(L, b)
                await_full(act, "P0", ("ott", L, b))
                if n >= 1:
                    await_full(act, "P1", ("proj", *back(L, b, 1)))
                act.activation(ONT[:], bank["P0"][:, 0:T], ACT.Copy).then_inc(ont_ok, 1)

            def copy_xd(b):
                await_full(act, "M0", ("dsm", 0, b))
                act.activation(xd[:, b, :, :].rearrange("c e n -> c (e n)"), bank["M0"][:, 0:NSLOT], ACT.Copy)\
                    .then_inc(xd_ok, 1)

            def copy_gt(b, k):
                if k == 0:
                    await_full(act, "M1", ("gt", 0, b, 0))
                    n = GCH[0][1] * CAP
                    act.activation(GT[0:n, b, 0:2, :], bank["M1"][0:n, :].rearrange("n (k q) -> n k q", k=2), ACT.Copy)\
                        .then_inc(gt_ok, 1)
                else:
                    await_full(act, "M0", ("gt", 0, b, 1))
                    n = GCH[2][1] * CAP
                    act.activation(GT[0:n, b, 2, :], bank["M0"][0:n, 0:T], ACT.Copy)\
                        .then_inc(gt_ok, 1)

            def copy_ys(b):
                await_full(act, f"M{b % 2}", ("py", 1, b))
                if b >= 1:
                    await_full(act, f"M{(b - 1) % 2}", ("po", 1, b - 1))
                for j, (_, ne) in ((0, GCH[0]), (2, GCH[2])):
                    n, k = ne * CAP, 2 if j == 0 else 1
                    last = act.activation(ys[0:n, j:j + k, :],
                                          bank[f"M{b % 2}"][0:n, P * j:P * (j + k)].rearrange("n (k c) -> n k c", k=k), ACT.Copy)
                last.then_inc(ys_ok, 1)

            def copy_xt(b):
                await_full(act, f"M{b % 2}", ("px", 1, b))
                act.activation(XT[:, T * b:T * (b + 1)], bank[f"M{b % 2}"][:, 0:T], ACT.Copy).then_inc(xt_ok, 1)

            def attention(plan):
                for item in plan:
                    k = item[0]
                    if k == "hi":
                        high(*item[1:])
                    if k == "exp":
                        exps(*item[1:])
                    if k == "mrow":
                        max_high(*item[1:])
                    if k == "ocp":
                        copy_o(*item[1:])
                    if k == "oev":
                        copy_ont(*item[1:])
                    if k == "dse":
                        copy_xd(item[2])
                    if k == "gte":
                        copy_gt(*item[2:])
                    if k == "py":
                        copy_ys(item[2])
                    if k == "px":
                        copy_xt(item[2])
                    if k == "bias1":
                        bias1()
                    if k == "route":
                        route()
                    if k == "route1":
                        route1()

            attention(plan0)
            act.wait_ge(bcol_ok, 7)
            with act.Fori(0, E0 - 1, 2) as e0:
                for i in range(2):
                    act.activation(ucol[i][:], b1T[:, bass.ds((e0 + i) * HC, HC)], ACT.Copy).then_inc(ucol_ok, 1)
                    act.wait_ge(ucol_ok, e0 + (i + 1))
                    for m in range(HC):
                        act.wait_ge(up_full, HC * (e0 + i) + (m + 1))
                        act.activation(F_H[i][:, NSLOT * m:NSLOT * (m + 1)],
                                       bank[f"{'NS'[m // 2]}{m % 2}"][:, 0:NSLOT], ACT.Relu,
                                       bias=ucol[i][:, m:m + 1]).then_inc(h_ok, 1)
            attention(plan1)
            await_full(act, "S1", ("st", 1, NB - 1, 3, 2))
            for g in range(4):
                act.activation(XH[:, 512 * g:512 * (g + 1)], XT[:, 512 * g:512 * (g + 1)], ACT.Copy).then_inc(xh_ok, 1)
            for g in range(4):
                act.wait_ge(gT_full, g + 1)
                act.activation(gT[:, 512 * g:512 * (g + 1)], bank[f"N{g % 2}"][0:E1, :], ACT.Copy).then_inc(gT_ok, 1)
            attention(tail1)
            act.sem_inc(gu_ok, 4)

            def weights(e, i):
                act.wait_ge(wt_full, 2 * e + 1)
                act.activation(WH[i], bank["M0"][:], ACT.Copy).then_inc(wh_ok, 1)

            def expert(e, i, more):
                act.activation(ucol[i][:], u1T[:, bass.ds(e * HC, HC)], ACT.Copy).then_inc(ucol_ok, 1)
                act.wait_ge(ucol_ok, e + (E0 + 1))
                for tc in range(4):
                    for m in range(HC):
                        act.wait_ge(gu_full, 16 * e + (4 * tc + m + 1))
                        act.activation(D_H[tc % 2][:, 512 * m:512 * (m + 1)], bank[f"{'NS'[m // 2]}{m % 2}"][:],
                                       ACT.Gelu, bias=ucol[i][:, m:m + 1]).then_inc(gu_ok, 1)
                if more:
                    weights(e + 1, 1 - i)

            weights(0, 0)
            with act.Fori(0, E1 - 3, 2) as e0:
                for i in range(2):
                    expert(e0 + i, i, True)
            for i in range(2):
                expert(E1 - 2 + i, i, i == 0)

        @block.vector
        def _(dve):
            chain = [0]

            def link(ins):
                chain[0] += 1
                ins.then_inc(dstep, 1)
                dve.wait_ge(dstep, chain[0])

            for i in range(NV):
                last = dve.memset(VA[i][:], 0.0)
            link(last)
            for i in range(NV):
                dve.memset(VA[i][:, :, :, HD:HD + 1], 1.0).then_inc(va_ok, 1)
            dve.wait_ge(x0_in, 16)
            for i in range(NT):
                if i == 4:
                    dve.wait_ge(x_in, 16)
                last = dve.bn_stats(stats[:, i, :], X[:, i, :])
            link(last)
            for i in range(NT):
                last = dve.bn_aggr(mv[:, i, :], stats[:, i, :])
            last.then_inc(mv_ok, 1)
            dve.wait_ge(mv_ok, 1)
            dve.wait_ge(k_in, 16)
            for dst, at in ((identb, CO_ID), (maskb, CO_MASK), (trib, CO_TRI), (oneb, CO_ONE)):
                last = dve.tensor_copy(dst[:], K[:, at:at + P])
            last.then_inc(const_ok, 1)
            dve.wait_ge(rstd_ok, 1)
            for i in range(NT):
                dve.tensor_scalar(XN[:, i, :], X[:, i, :], mv[:, i, 0:1], rstd[:, i:i + 1], ALU.subtract, ALU.mult)\
                    .then_inc(xn_ok, 1)

            def top2():
                for i in range(NT):
                    last = dve.max(top[:, i, :], lg[:, i, :])
                link(last)
                for i in range(NT):
                    last = dve.max_index(tix[:, i, :], top[:, i, :], lg[:, i, :])
                link(last)
                link(dve.tensor_copy(tif[:], tix[:, :, 0:2]))
                for k in range(2):
                    last = dve.tensor_tensor(oh[:, :, k, :], K[:, None, CO_I8:CO_I8 + E0].broadcast_to((P, NT, E0)),
                                             tif[:, :, k:k + 1].broadcast_to((P, NT, E0)), ALU.is_equal)
                link(last)

            def route():
                await_full(dve, "P0", ("lg",))
                dve.tensor_copy(lg[:].rearrange("p a e -> p (a e)"), bank["P0"][:, 0:NT * E0]).then_inc(lg_ok, 1)
                dve.wait_ge(lg_ok, 1)
                top2()
                link(dve.tensor_tensor(sel[:], oh[:, :, 0, :], oh[:, :, 1, :], ALU.add))
                dve.tensor_copy(selb[:], sel[:]).then_inc(sel_ok, 1)
                dve.tensor_tensor(dlt[:], lg[:], top[:, :, 0:1].broadcast_to((P, NT, E0)), ALU.subtract)\
                    .then_inc(exin_ok, 1)
                dve.wait_ge(ex_ok, 1)
                link(dve.tensor_reduce(zs[:], ex[:], AX.X, ALU.add))
                link(dve.reciprocal(rz[:], zs[:]))
                dve.tensor_tensor(gate[:], ex[:], rz[:, :, None].broadcast_to((P, NT, E0)), ALU.mult).then_inc(gate_ok, 1)

            def keys():
                await_full(dve, "P1", ("cum",))
                dve.scalar_tensor_tensor(out=key[:].rearrange("p a e -> p (a e)"), in0=bank["P1"][:, 0:NT * E0],
                                         scalar=1.0, in1=sel[:].rearrange("p a e -> p (a e)"),
                                         op0=ALU.add, op1=ALU.mult).then_inc(key_ok, 1)
                dve.wait_ge(key_ok, 1)

            def row_max(L, b, u):
                n = seq(L, b)
                if u == 0 and n >= 2:
                    await_full(dve, "M1", ("mxt", *back(L, b, 2), 1))
                h, v = u // 6, u % 6
                qt, p, heads = nat_heads(h, v)
                many, first = len(heads), heads[0] // 2 % 4
                s = f"N{u % 2}"
                await_full(dve, s, ("nat", L, b, u))
                dve.tensor_reduce(NM[b % 2][:, h, qt, :].rearrange("q (j p) -> q p j", p=2)[:, p, first:first + many],
                                  bank[s][:].rearrange("q (h k) -> q h k", h=many), AX.X, ALU.max, negate=True)\
                    .then_inc(nm_ok, 1)

            def low(L, b):
                n, i = seq(L, b), b % 2
                dve.wait_ge(qhi_ok, n + 1)
                if L == 0:
                    for j in range(2):
                        last = dve.scalar_tensor_tensor(out=XQ[i][:, 2 * j + 1, :], in0=bank["M1"][:, j * T:(j + 1) * T],
                                                        scalar=bcol[:, j:j + 1], in1=XQ[i][:, 2 * j, :].bitcast(F32),
                                                        op0=ALU.add, op1=ALU.subtract)
                    last.then_inc(qlo_ok, 1)
                else:
                    for j, rows in ((0, P), (2, NKV * HD)):
                        last = dve.tensor_tensor(XQ[i][0:rows, j + 1, :], ROT[i][0:rows, j, :],
                                                 XQ[i][0:rows, j, :].bitcast(F32), ALU.subtract)
                    last.then_inc(qlo_ok, 1)

            def rotary(b):
                i = b % 2
                if b >= 2:
                    dve.wait_ge(qlo_ok, NB + b - 1)
                dve.wait_ge(rc_ok, 1)
                for j, (n, rows, col) in enumerate((("M1", P, 2), ("M0", NKV * HD, 4))):
                    await_full(dve, n, ("qk", 1, b))
                    for a, tab in ((0, cosr), (1, sinr)):
                        last = dve.scalar_tensor_tensor(out=ROT[i][0:rows, 2 * j + a, :],
                                                        in0=bank[n][0:rows, a * T:(a + 1) * T],
                                                        scalar=bcol[0:rows, col + a:col + a + 1], in1=tab[0:rows, :],
                                                        op0=ALU.add, op1=ALU.mult)
                last.then_inc(rot_ok, 1)

            def values(L, b):
                n = seq(L, b)
                nk = NH if L == 0 else NKV
                await_full(dve, "M0", ("val", L, b))
                if n == 0:
                    dve.wait_ge(va_ok, NV)
                    dve.wait_ge(wo_in, 16 * 6)
                if n >= NV:
                    dve.wait_ge(pv_ok, 4 * (n - NV + 1) if b >= NV else 4 * NB)
                dve.tensor_tensor(VA[b % NV][:, :, 0:nk, 0:HD],
                                  bank["M0"][:, 0:TPB * nk * HD].rearrange("k (t h d) -> k t h d", t=TPB, h=nk),
                                  bvb[L][:, 0:nk * HD].rearrange("k (h d) -> k h d", h=nk)[:, None, :, :]
                                  .broadcast_to((P, TPB, nk, HD)), ALU.add).then_inc(val_ok, 1)

            def max_low(L, b, h):
                n = 2 * seq(L, b) + h
                dve.wait_ge(mhi_ok, n + 1)
                dve.tensor_tensor(MS[h][:, 1, :], bank["M1"][0:NH // 2, 0:T], MS[h][:, 0, :].bitcast(F32), ALU.subtract)\
                    .then_inc(mlo_ok, 1)

            def normalise(L, b):
                n = seq(L, b)
                for q in range(TPB):
                    await_full(dve, f"P{q}", ("otr", L, b, q))
                    o = bank[f"P{q}"][:].rearrange("q (h w) -> q h w", w=32)
                    link(dve.reciprocal(rcp[:, q, :, None], o[:, :, HD:HD + 1]))
                    if n >= 1 and q == 0:
                        await_full(dve, "P0", ("ott", *back(L, b, 1)))
                    dve.tensor_tensor(ON[:, q, :].rearrange("q (h d) -> q h d", h=NH), o[:, :, 0:HD],
                                      rcp[:, q, :, None].broadcast_to((P, NH, HD)), ALU.mult).then_inc(on_ok, 1)

            def residual(L, b):
                n = seq(L, b)
                await_full(dve, "P1", ("proj", L, b))
                if L == 0:
                    dve.wait_ge(xbo_ok, 1)
                else:
                    dve.wait_ge(ybo_ok, b + 1)
                dve.tensor_tensor(X[:, 2 * b:2 * b + 2, :], bank["P1"][:, 0:T].rearrange("q (t c) -> q t c", t=2),
                                  X[:, 2 * b:2 * b + 2, :], ALU.add).then_inc(x1_ok, 1)

            def dispatch(b):
                if b > 0:
                    await_full(dve, "M0", ("dsm", 0, b - 1))
                    dve.wait_ge(gm_ok, b)
                for q in range(TPB):
                    last = dve.tensor_tensor(DM[:, q, :, :], K[:, None, CO_IN:CO_IN + CAP].broadcast_to((P, E0, CAP)),
                                             key[:, 2 * b + q, :, None].broadcast_to((P, E0, CAP)), ALU.is_equal)
                last.then_inc(dm_ok, 1)

            def router_constants():
                dve.wait_ge(f_in, 16 * 17)
                dve.tensor_scalar(rwS[:], rwS[:], lns[:, 0:1], None, ALU.mult).then_inc(rcin_ok, 1)
                dve.tensor_scalar(rwB[:], rwB[:], lnb[:, 0:1], None, ALU.mult).then_inc(rcin_ok, 1)
                await_full(dve, "M0", ("rcon",))
                dve.tensor_copy(rc[:, 0, :], bank["M0"][:, 0:E1])
                dve.tensor_tensor(rc[:, 1, :], bank["M0"][:, E1:2 * E1], rbb[:], ALU.add).then_inc(rc_ok, 1)

            def combine(b):
                s = slice(2 * b, 2 * b + 2)
                await_full(dve, f"M{b % 2}", ("po", 1, b))
                dve.wait_ge(x1_ok, b + 1)
                dve.tensor_tensor(X[:, s, :], bank[f"M{b % 2}"][:, 0:T].rearrange("q (t c) -> q t c", t=2), X[:, s, :],
                                  ALU.add)\
                    .then_inc(x2_ok, 1)
                dve.wait_ge(x2_ok, b + 1)
                for i in (2 * b, 2 * b + 1):
                    last = dve.bn_stats(stats[:, i, :], X[:, i, :])
                link(last)
                for i in (2 * b, 2 * b + 1):
                    last = dve.bn_aggr(mv[:, i, :], stats[:, i, :])
                last.then_inc(mvb_ok, 1)

            def normalise_x(b):
                dve.wait_ge(mvb_ok, b + 1)
                dve.wait_ge(rstdb_ok, b + 1)
                for i in (2 * b, 2 * b + 1):
                    dve.tensor_scalar(XN[:, i, :], X[:, i, :], mv[:, i, 0:1], rstd[:, i:i + 1], ALU.subtract, ALU.mult)\
                        .then_inc(xnb_ok, 1)
                dve.wait_ge(xnb_ok, 2 * b + 2)
                for i in (2 * b, 2 * b + 1):
                    last = dve.bn_stats(stats2[:, i, :], XN[:, i, :])
                link(last)
                for i in (2 * b, 2 * b + 1):
                    last = dve.bn_aggr(mv2[:, i, :], stats2[:, i, :])
                last.then_inc(mvc_ok, 1)

            def logits(b):
                s = slice(2 * b, 2 * b + 2)
                await_full(dve, f"M{b % 2}", ("pl", 1, b))
                dve.tensor_copy(lg[:, s, :].rearrange("p a e -> p (a e)"), bank[f"M{b % 2}"][:, 0:2 * E1]).then_inc(lg1_ok, 1)

            def route1():
                dve.wait_ge(rstdc_ok, NB)
                dve.wait_ge(mvc_ok, NB)
                dve.wait_ge(rc_ok, 1)
                dve.wait_ge(lg1_ok, NB)

                def bc(x):
                    return x.broadcast_to((P, NT, E1))
                link(dve.tensor_tensor(dlt[:], bc(mv2[:, :, 0:1]), bc(rc[:, 0:1, :]), ALU.mult))
                link(dve.tensor_tensor(ex[:], lg[:], dlt[:], ALU.subtract))
                link(dve.tensor_tensor(dlt[:], ex[:], bc(rstd2[:, :, None]), ALU.mult))
                link(dve.tensor_tensor(lg[:], dlt[:], bc(rc[:, 1:2, :]), ALU.add))
                top2()
                link(dve.tensor_tensor(tif[:], top[:, :, 0:2], top[:, :, 0:1].broadcast_to((P, NT, 2)), ALU.subtract))
                dve.sem_inc(exin_ok, 1)
                dve.wait_ge(ex_ok, 2)
                link(dve.tensor_reduce(zs[:], top[:, :, 2:4], AX.X, ALU.add))
                link(dve.reciprocal(rz[:], zs[:]))
                link(dve.tensor_tensor(tif[:], top[:, :, 2:4], rz[:, :, None].broadcast_to((P, NT, 2)), ALU.mult))
                for k in range(2):
                    last = dve.tensor_tensor((sel if k == 0 else dlt)[:], oh[:, :, k, :], bc(tif[:, :, k:k + 1]), ALU.mult)
                link(last)
                link(dve.tensor_tensor(gate[:], sel[:], dlt[:], ALU.add))
                dve.sem_inc(g1_ok, 1)

            def attention(plan):
                for item in plan:
                    k = item[0]
                    if k == "max":
                        row_max(*item[1:])
                    if k == "lo":
                        low(*item[1:])
                    if k == "qk" and item[1] == 1:
                        rotary(item[2])
                    if k == "vev":
                        values(*item[1:])
                    if k == "mrow":
                        max_low(*item[1:])
                    if k == "norm":
                        normalise(*item[1:])
                    if k == "res":
                        residual(*item[1:])
                    if k == "disp":
                        dispatch(item[2])
                    if k == "rcon":
                        router_constants()
                    if k == "route":
                        route()
                    if k == "route1":
                        route1()
                    if k == "keys":
                        keys()
                    if k == "po":
                        combine(item[2])
                    if k == "px":
                        normalise_x(item[2])
                    if k == "pl":
                        logits(item[2])

            attention(plan0)
            dve.wait_ge(bcol_ok, 7)
            dve.sem_inc(y_ok, 2)
            with dve.Fori(0, E0 - 1, 2) as e0:
                for i in range(2):
                    dve.wait_ge(y_full, e0 + (i + 1))
                    dve.tensor_scalar(xd[:, :, bass.ds(e0 + i, 1), :].rearrange("c b e n -> c b (e n)"),
                                      bank[f"M{i}"][:, 0:NSLOT].rearrange("c (b n) -> c b n", b=NB),
                                      b2T[:, bass.ds(e0 + i, 1)], None, ALU.add).then_inc(y_ok, 1)
            attention(plan1)
            for g in range(4):
                dve.wait_ge(xh_ok, g + 1)
                dve.tensor_tensor(XL[:, 512 * g:512 * (g + 1)], XT[:, 512 * g:512 * (g + 1)],
                                  XH[:, 512 * g:512 * (g + 1)].bitcast(F32), ALU.subtract).then_inc(xl_ok, 1)
            for g in range(4):
                dve.wait_ge(b2_full, g + 1)
                last = dve.tensor_tensor(X[:, 4 * g:4 * g + 4, :], bank[f"S{g % 2}"][:].rearrange("q (t c) -> q t c", t=4),
                                         X[:, 4 * g:4 * g + 4, :], ALU.add)
                last.then_inc(b2_ok, 1)
            dve.wait_ge(b2_ok, 4)
            attention(tail1)
            dve.wait_ge(x1_ok, 2 * NB)
            dve.sem_inc(gy_free, 2)
            def weights(e, i):
                dve.wait_ge(wh_ok, e + 1)
                dve.tensor_tensor(WL[i], bank["M0"][:], WH[i].bitcast(F32), ALU.subtract).then_inc(wt_ok, 1)
                dve.wait_ge(wt_full, 2 * e + 2)
                dve.tensor_copy(D_W[i][:], bank["M1"][:]).then_inc(wt_ok, 1)

            def expert(e, i, more):
                for tc in range(4):
                    if tc == 3 and more:
                        weights(e + 1, 1 - i)
                    dve.wait_ge(gy_full, 4 * e + (tc + 1))
                    for tt in range(4):
                        x = X[:, 4 * tc + tt, :]
                        last = dve.scalar_tensor_tensor(out=x, in0=bank[f"P{tc % 2}"][:, P * tt:P * (tt + 1)],
                                                        scalar=gate[:, 4 * tc + tt, bass.ds(e, 1)], in1=x,
                                                        op0=ALU.mult, op1=ALU.add)
                    last.then_inc(gy_free, 1)

            weights(0, 0)
            with dve.Fori(0, E1 - 3, 2) as e0:
                for i in range(2):
                    expert(e0 + i, i, True)
            for i in range(2):
                expert(E1 - 2 + i, i, i == 0)

        @block.tensor
        def _(pe):
            mm = pe.matmul
            M0, M1 = bank["M0"], bank["M1"]
            one = ones[0:1, 0:1]
            pe.wait_ge(k_in, 16)
            pe.wait_ge(brow_ok, 64)
            for i in range(2):
                last = mm(M0[:, i:i + 1], brow[0:1, i, :], one, start=True, stop=True)
            last.then_inc(full["M0"], 1)
            for i in range(4):
                n = f"{'NNSS'[i]}{i % 2}"
                pe.wait_ge(xn_ok, 4 * (i + 1))
                for j in range(4):
                    last = pe.transpose(bank[n][:, P * j:P * (j + 1)], XN[:, 4 * i + j, :], ident)
                last.then_inc(full[n], 1)
            pe.wait_ge(w_in, 64)
            pe.wait_ge(xt0_ok, 4)

            def router():
                for i in range(NT):
                    last = mm(bank["P0"][:, E0 * i:E0 * (i + 1)], XT[:, P * i:P * (i + 1)], Wr[:], start=True, stop=True)
                last.then_inc(full["P0"], 1)

            def bias1():
                await_free(pe, "M0", ("bias1",))
                pe.wait_ge(f_in, 16 * 17)
                pe.wait_ge(ab_ok, 1)
                mm(M0[:, 2:6], K[0:1, CO_MASK:CO_MASK + P], K[0:1, CO_TRI:CO_TRI + 1].broadcast_to((1, 4)),
                   start=True, stop=True)
                for i, n in enumerate((P, P, NKV * HD, NKV * HD)):
                    mm(M0[0:n, 2 + i:3 + i], browP[0:1, i, 0:n], one, start=True, stop=True)
                pe.transpose(M0[:, 32:64], b1raw[:], ident[0:32, 0:32])
                pe.transpose(M0[:, 64:96], u1raw[:], ident[0:32, 0:32])
                pe.transpose(M0[:, 96:104], b2raw[:], ident[0:E0, 0:E0])
                pe.transpose(M0[:, 104:112], rwr[:], ident[0:E1, 0:E1]).then_inc(full["M0"], 1)

            def cum():
                await_free(pe, "P1", ("cum",))
                pe.wait_ge(const_ok, 1)
                pe.wait_ge(sel_ok, 1)
                o = bank["P1"][:, 0:NT * E0]
                mm(o, trib[:], selb[:].rearrange("p a e -> p (a e)"), start=True, stop=False)
                mm(o.rearrange("p (b q e) -> p b q e", q=2, e=E0)[:, :, 1, :], oneb[:],
                   selb[:].rearrange("p (b q) e -> p b q e", q=2)[:, :, 0, :], start=False, stop=True)\
                    .then_inc(full["P1"], 1)

            def qk(L, b):
                x = XT[:, T * b:T * (b + 1)]
                if L == 0:
                    await_free(pe, "M1", ("qk", L, b))
                    for j in range(2):
                        last = mm(M1[:, T * j:T * (j + 1)], Wqkv[0][:, j, :], x, start=True, stop=True)
                    last.then_inc(full["M1"], 1)
                else:
                    await_free(pe, "M1", ("qk", L, b))
                    await_free(pe, "M0", ("qk", L, b))
                    for j in range(2):
                        last = mm(M1[:, T * j:T * (j + 1)], WqAB[:, j, :], x, start=True, stop=True)
                    last.then_inc(full["M1"], 1)
                    for j in range(2):
                        last = mm(M0[0:32, T * j:T * (j + 1)], WkAB[:, j, :], x, start=True, stop=True)
                    last.then_inc(full["M0"], 1)

            def val(L, b):
                n = C if L == 0 else NKV * HD
                await_free(pe, "M0", ("val", L, b))
                for q in range(TPB):
                    last = mm(M0[:, n * q:n * (q + 1)], XT[:, T * b + P * q:T * b + P * (q + 1)], Wqkv[L][:, 2, 0:n],
                              start=True, stop=True)
                last.then_inc(full["M0"], 1)

            def k_part(L, h):
                return 8 + (h // 2 if L == 0 else NKV * (h % 2) + h // (NH // NKV))

            def keep_clock(s):
                mm(s[:], identb[:], maskb[:, None, :].broadcast_to((P, 4, P)), start=True, stop=True,
                   skip_group_check=True)

            def nat(L, b, u):
                h, v = u // 6, u % 6
                qt, p, heads = nat_heads(h, v)
                many = len(heads)
                s = bank[f"N{u % 2}"]
                await_free(pe, f"N{u % 2}", ("nat", L, b, u))
                if u == 0:
                    pe.wait_ge(stk_in[b % NSTK], stack_in_count(L, b))
                w_ = 512 // many
                if L == 0 and u in WARM[0]:
                    keep_clock(s)
                diag = s[:].rearrange("q (h k) -> q h k", h=many)[:, :, w_ - P:w_]
                mm(diag, identb[:], maskb[:, None, :].broadcast_to((P, many, P)), start=True, stop=False,
                   skip_group_check=True)
                stk = STK[b % NSTK]
                for i, head in enumerate(heads):
                    j = head // 2
                    last = mm(s[:, w_ * i:w_ * (i + 1)], stk[64 * p:64 * p + 32, j, P * qt:P * (qt + 1)],
                              stk[64 * p:64 * p + 32, k_part(L, head), 0:w_], start=False, stop=True,
                              skip_group_check=True)
                last.then_inc(full[f"N{u % 2}"], 1)

            def stack_in_count(L, b):
                s = b % NSTK
                n0 = len([x for x in range(NB) if x % NSTK == s])
                k = b // NSTK + 1
                return 32 * k if L == 0 else 32 * n0 + 64 * k

            def m_in_count(L, b):
                s = b % NSTK
                n0 = len([x for x in range(NB) if x % NSTK == s])
                return 32 * (b // NSTK + 1 + (n0 if L else 0))

            def st(L, b, g, r):
                u = 3 * g + r
                s = bank[f"S{u % 2}"]
                await_free(pe, f"S{u % 2}", ("st", L, b, g, r))
                if r == 0 and g % 2 == 0:
                    pe.wait_ge(m_in[b % NSTK][g // 2], m_in_count(L, b))
                heads = group_heads(g)[2 * r:2 * r + 2] if r < 2 else group_heads(g)
                n = 512 // len(heads)
                if L == 1 and u in WARM[1]:
                    keep_clock(s)
                stk = STK[b % NSTK]
                m = 1 if L == 0 else 2
                for i, head in list(enumerate(heads))[::m]:
                    j, p = head // 2, head % 2
                    kt = 0 if r < 2 else 1
                    rows = slice(64 * p, 64 * p + 34) if L == 0 else slice(0, P)
                    last = mm(s[:, n * i:n * (i + m)], stk[rows, k_part(L, head), P * kt:P * (kt + 1)],
                              stk[rows, j:j + m, T - n:T], start=True, stop=True)
                last.then_inc(full[f"S{u % 2}"], 1)

            def pv(L, b, g):
                n = seq(L, b)
                bk = f"P{g // 2}"
                if g % 2 == 0:
                    await_free(pe, bk, ("o", L, b, g // 2))
                if g == 0:
                    pe.wait_ge(val_ok, n + 1)
                pe.wait_ge(mask_ok, 4 * n + g + 1)
                va = VA[b % NV]
                for kt in range(2):
                    for c in range(4):
                        head = group_heads(g)[c] // (1 if L == 0 else NH // NKV)
                        o = bank[bk][32 * c:32 * c + 32, T * (g % 2) + P * kt:T * (g % 2 + 1)]
                        pr = PT[:, g, c // 2, T * (c % 2):T * (c % 2 + 1)] if kt == 0 else PT[:, g, 2, P * c:P * (c + 1)]
                        last = mm(o, va[:, kt, head, :], pr, start=(kt == 0), stop=(kt == 1))
                last.then_inc(pv_ok, 1)

            def mxt(L, b, h):
                n = seq(L, b)
                await_free(pe, "M1", ("mxt", L, b, h))
                pe.wait_ge(nm_ok, 12 * n + 6 * (h + 1))
                for q in range(TPB):
                    last = pe.transpose(M1[0:8, P * q:P * (q + 1)], NM[b % 2][:, h, q, :], ident)
                last.then_inc(full["M1"], 1)

            def otr(L, b):
                n = seq(L, b)
                pe.wait_ge(ocp_ok, 2 * n + 2)
                for q in range(TPB):
                    await_free(pe, f"P{q}", ("otr", L, b, q))
                    for g in range(4):
                        last = pe.transpose(bank[f"P{q}"][:, P * g:P * (g + 1)],
                                            OT[b % 2][:, T * g + P * q:T * g + P * (q + 1)], ident)
                    last.then_inc(full[f"P{q}"], 1)

            def ott(L, b):
                n = seq(L, b)
                await_free(pe, "P0", ("ott", L, b))
                pe.wait_ge(on_ok, 2 * n + 2)
                for q in range(TPB):
                    last = pe.transpose(bank["P0"][:, P * q:P * (q + 1)], ON[:, q, :], ident)
                last.then_inc(full["P0"], 1)

            def proj(L, b):
                n = seq(L, b)
                await_free(pe, "P1", ("proj", L, b))
                pe.wait_ge(ont_ok, n + 1)
                if n == 0:
                    pe.wait_ge(wo_in, 16 * 6)
                for q in range(TPB):
                    last = mm(bank["P1"][:, P * q:P * (q + 1)], ONT[:, P * q:P * (q + 1)], Wo[L][:], start=True, stop=True)
                last.then_inc(full["P1"], 1)

            def dsm(b):
                await_free(pe, "M0", ("dsm", 0, b))
                pe.wait_ge(dm_ok, b + 1)
                for q in range(TPB):
                    last = mm(M0[:, 0:NSLOT], XN[:, 2 * b + q, :], DM[:, q, :, :].rearrange("p e n -> p (e n)"),
                              start=(q == 0), stop=(q == 1))
                last.then_inc(full["M0"], 1)

            def gt(b, k):
                bk = "M1" if k == 0 else "M0"
                await_free(pe, bk, ("gt", 0, b, k))
                pe.wait_ge(gm_ok, b + 1)
                for j, (e, ne) in enumerate(GCH[:2] if k == 0 else GCH[2:]):
                    at, n = e * CAP, ne * CAP
                    for q in range(TPB):
                        last = pe.transpose(bank[bk][0:n, T * j + P * q:T * j + P * (q + 1)],
                                            GM[:, q, :, :].rearrange("p e n -> p (e n)")[:, at:at + n], ident)
                last.then_inc(full[bk], 1)

            def rcon():
                await_free(pe, "M0", ("rcon",))
                pe.wait_ge(rcin_ok, 2)
                mm(M0[:, 0:E1], ones, rwS[:], start=True, stop=True)
                mm(M0[:, E1:2 * E1], ones, rwB[:], start=True, stop=True).then_inc(full["M0"], 1)

            def slots_out(b):
                m = f"M{b % 2}"
                await_free(pe, m, ("py", 1, b))
                for j, (e, ne) in enumerate(GCH):
                    last = pe.transpose(bank[m][0:ne * CAP, P * j:P * (j + 1)], xd[:, b, e:e + ne, :].rearrange("c e n -> c (e n)"),
                                        ident)
                last.then_inc(full[m], 1)

            def combine(b):
                m = f"M{b % 2}"
                await_free(pe, m, ("po", 1, b))
                pe.wait_ge(ys_ok, b + 1)
                for q in range(TPB):
                    for j, n in enumerate(ne * CAP for _, ne in GCH):
                        last = mm(bank[m][:, P * q:P * (q + 1)], GT[0:n, b, j, P * q:P * (q + 1)], ys[0:n, j, :],
                                  start=(j == 0), stop=(j == 2))
                last.then_inc(full[m], 1)

            def xt(b):
                m = f"M{b % 2}"
                await_free(pe, m, ("px", 1, b))
                pe.wait_ge(xnb_ok, 2 * b + 2)
                for q in range(TPB):
                    last = pe.transpose(bank[m][:, P * q:P * (q + 1)], XN[:, 2 * b + q, :], ident)
                last.then_inc(full[m], 1)

            def logits(b):
                m = f"M{b % 2}"
                await_free(pe, m, ("pl", 1, b))
                pe.wait_ge(xt_ok, b + 1)
                for q in range(TPB):
                    last = mm(bank[m][:, E1 * q:E1 * (q + 1)], XT[:, T * b + P * q:T * b + P * (q + 1)], rwS[:],
                              start=True, stop=True)
                last.then_inc(full[m], 1)

            layer1 = {"py": slots_out, "po": combine, "px": xt, "pl": logits}
            work = {"qk": qk, "val": val, "nat": nat, "st": st, "pv": pv, "mxt": mxt, "otr": otr, "ott": ott,
                    "proj": proj}

            def attention(plan):
                for item in plan:
                    k = item[0]
                    if k in work:
                        work[k](*item[1:])
                    if k == "dsm":
                        dsm(item[2])
                    if k == "gt":
                        gt(*item[2:])
                    if k == "rcon":
                        rcon()
                    if k in layer1:
                        layer1[k](item[2])
                    if k == "bias1":
                        bias1()
                    if k == "lg":
                        router()
                    if k == "cum":
                        cum()

            attention(plan0)

            for n in names[:4] + names[6:]:
                pe.wait_ge(*released(last0[n]))
            pe.wait_ge(xd_ok, NB)
            with pe.Fori(0, E0 - 1, 2) as e0:
                for i in range(2):
                    pe.wait_ge(fw_in[i], 16 * e0 + 32)
                    x = xd[:, :, bass.ds(e0 + i, 1), :].rearrange("c b e n -> c b (e n)")
                    for m in range(HC):
                        last = mm(bank[f"{'NS'[m // 2]}{m % 2}"][:, 0:NSLOT], F_W[i][:, P * m:P * (m + 1)], x,
                                  start=True, stop=True)
                        last.then_inc(up_full, 1)
                    pe.wait_ge(y_ok, e0 + (i + 1))
                    for m in range(HC):
                        pe.wait_ge(h_ok, HC * (e0 + i) + (m + 1))
                        last = mm(bank[f"M{i}"][:, 0:NSLOT], F_W[i][:, H0 + P * m:H0 + P * (m + 1)],
                                  F_H[i][:, NSLOT * m:NSLOT * (m + 1)], start=(m == 0), stop=(m == HC - 1))
                    last.then_inc(y_full, 1)
            pe.wait_ge(y_ok, E0 + 2)
            attention(plan1)

            for n in names[:4] + names[6:]:
                pe.wait_ge(*released(last_use[n]))
            pe.wait_ge(g1_ok, 1)
            for g in range(4):
                if g >= 2:
                    pe.wait_ge(gT_ok, g - 1)
                for j in range(4):
                    last = pe.transpose(bank[f"N{g % 2}"][0:E1, P * j:P * (j + 1)], gate[:, 4 * g + j, :], ident)
                last.then_inc(gT_full, 1)
            for g in range(4):
                pe.wait_ge(gT_ok, g + 1)
                if g >= 2:
                    pe.wait_ge(b2_ok, g - 1)
                for j in range(4):
                    i = 4 * g + j
                    last = mm(bank[f"S{g % 2}"][:, P * j:P * (j + 1)], gT[:, P * i:P * (i + 1)], d2row[:],
                              start=True, stop=True)
                last.then_inc(b2_full, 1)
            attention(tail1)
            pe.wait_ge(b2_ok, 4)
            for n in names[4:6]:
                pe.wait_ge(*released(last_use[n]))
            def weights(e, i, loads):
                pe.wait_ge(dw_in[i], loads)
                for h in range(2):
                    for m in range(HC):
                        src = D_RAW[i][:, 512 * h + P * m:512 * h + P * (m + 1)]
                        last = pe.transpose(bank[f"M{h}"][:, P * m:P * (m + 1)], src, ident)
                    last.then_inc(wt_full, 1)

            def up(e, i, tc):
                if tc == 0:
                    pe.wait_ge(wt_ok, 2 * e + 2)
                for m in range(HC):
                    pe.wait_ge(gu_ok, 16 * e + (4 * tc + m + 1))
                    at, x = slice(P * m, P * (m + 1)), slice(512 * tc, 512 * (tc + 1))
                    o = bank[f"{'NS'[m // 2]}{m % 2}"][:]
                    mm(o, WH[i][:, at], XH[:, x], start=True, stop=False)
                    mm(o, WH[i][:, at], XL[:, x], start=False, stop=False)
                    mm(o, WL[i][:, at], XH[:, x], start=False, stop=True).then_inc(gu_full, 1)

            def down(e, i, tc):
                pe.wait_ge(gu_ok, 16 * e + (4 * tc + 8))
                pe.wait_ge(gy_free, 4 * e + (tc + 1))
                for tt in range(4):
                    for m in range(HC):
                        last = mm(bank[f"P{tc % 2}"][:, P * tt:P * (tt + 1)],
                                  D_H[tc % 2][:, 512 * m + P * tt:512 * m + P * (tt + 1)],
                                  D_W[i][:, P * m:P * (m + 1)], start=(m == 0), stop=(m == HC - 1))
                last.then_inc(gy_full, 1)

            def expert(e, i, more, loads):
                up(e, i, 0)
                for tc in range(4):
                    if tc < 3:
                        up(e, i, tc + 1)
                    elif more:
                        weights(e, 1 - i, loads)
                    down(e, i, tc)

            pe.wait_ge(xl_ok, 4)
            weights(0, 0, 32)
            with pe.Fori(0, E1 - 3, 2) as e0:
                for i in range(2):
                    expert(e0 + i, i, True, 16 * e0 + 32 * (i + 1))
            for i in range(2):
                expert(E1 - 2 + i, i, i == 0, 16 * (E1 - 2) + 32 * (i + 1))


def kernel(**inputs):
    import concourse.bacc as bacc
    from concourse.bass_utils import run_bass_kernel_spmd

    nc = bacc.Bacc("TRN2", target_bir_lowering=False, num_devices=1)
    arrays, aps = {}, {}
    for name in INPUTS:
        a = np.ascontiguousarray(inputs[name])
        arrays[f"in_{name}"] = a
        aps[name] = nc.dram_tensor(f"in_{name}", a.shape, mybir.dt.from_np(a.dtype), kind="ExternalInput").ap()
    arrays["in_table"] = constants()
    table = nc.dram_tensor("in_table", (P, NCONST), F32, kind="ExternalInput").ap()
    out = nc.dram_tensor("out_0", (NB, T, C), F32, kind="ExternalOutput").ap()
    build(nc, aps, table, out)
    r = run_bass_kernel_spmd(nc, [arrays], core_ids=[0])
    return r.results[0]["out_0"]
```
